# Optimizing a Trainium2 kernel written in Bass

```python
import numpy as np
import jax
import jax.numpy as jnp

def _softmax(x, axis=-1):
    return jax.nn.softmax(x, axis=axis)

def _gelu(x):
    return jax.nn.gelu(x, approximate=True)

def _silu(x):
    return jax.nn.silu(x)

def _sigmoid(x):
    return jax.nn.sigmoid(x)

def _layernorm(x, axis=-1, eps=1e-05):
    m = jnp.mean(x, axis=axis, keepdims=True)
    v = jnp.var(x, axis=axis, keepdims=True)
    return (x - m) / jnp.sqrt(v + eps)

def _scatter_add(tgt, idx, src, axis=0):
    return tgt.at[idx].add(src)

def _segment_sum(src, seg, n):
    return jax.ops.segment_sum(src, seg, n)
kernel_name = 'mk_cond_resid_d2_seqx_r2_49079a'

def setup_inputs(seed: int=0):
    np.random.seed(seed)
    _w = jnp.asarray

    def _rec_inputs():
        import jax
        import jax.numpy as jnp
        _rk = jax.random.key(seed)
        x = -0.0003929 + 0.9999 * jax.random.normal(jax.random.fold_in(_rk, 1), (2, 2048, 512), jnp.float32)
        _lenS = 2048 - jax.random.randint(jax.random.fold_in(_rk, 7), (2,), 0, max(1, 2048 // 4) + 1, jnp.int32)
        _lenS2 = 2048 - jax.random.randint(jax.random.fold_in(_rk, 8), (2,), 0, max(1, 2048 // 4) + 1, jnp.int32)
        itok_B_0_7 = jax.random.randint(jax.random.fold_in(_rk, 11), (2,), 0, 8, jnp.int32)
        condB_tauraws = -5.74692 + 0.777674 * jax.random.normal(jax.random.fold_in(_rk, 12), (2,), jnp.float32)
        cond_256 = -0.000235209 + 0.019331 * jax.random.normal(jax.random.fold_in(_rk, 13), (2, 128), jnp.float32)
        condB_bn2 = jnp.zeros((2,), jnp.float32)
        cond_1024 = -4.10585e-05 + 0.0199478 * jax.random.normal(jax.random.fold_in(_rk, 15), (2, 512), jnp.float32)
        return (x, itok_B_0_7, condB_tauraws, cond_256, condB_bn2, cond_1024)
    x, itok_B_0_7, condB_tauraws, cond_256, condB_bn2, cond_1024 = _rec_inputs()

    def _L0_cond_setup():
        import jax, jax.numpy as jnp
        import numpy as np
        S, O, H = (8, 512, 512)
        B, N = (32, 256)
        key = jax.random.key(seed)
        k1, k2, k3, k4 = jax.random.split(key, 4)
        x = jax.random.normal(k1, (B, N, H), dtype=jnp.float32)
        subject_id = jax.random.randint(k2, (B,), 0, S)
        wbound = jnp.sqrt(2.0 / 6.0) * jnp.sqrt(3.0 / H)
        weight = jax.random.uniform(k3, (S, O, H), minval=-wbound, maxval=wbound, dtype=jnp.float32)
        bbound = 1.0 / jnp.sqrt(H)
        bias = jax.random.uniform(k4, (S, O), minval=-bbound, maxval=bbound, dtype=jnp.float32)
        return {'x': x, 'subject_id': subject_id, 'weight': weight, 'bias': bias}
    _L0_cond_all = _L0_cond_setup()
    _L0_cond_in = {k: v for k, v in _L0_cond_all.items() if k in ('weight', 'bias')}
    del _L0_cond_all

    def _L1_cond_setup():
        import jax, jax.numpy as jnp
        import numpy as np
        import math
        B, T, E, D = (4, 1024, 512, 4)

        def _tau_init(t):
            a = 0.1 ** (1.0 / max(t - 1, 1))
            tt = -math.log(max(a, 1e-10))
            return math.log(math.exp(tt) - 1 + 1e-10)

        def causal_ema(b, tau_raw):
            alpha = jnp.exp(-jax.nn.softplus(tau_raw)).astype(b.dtype)

            def step(h, bt):
                h = alpha * h + bt
                return (h, h)
            h0 = jnp.zeros((b.shape[0], b.shape[2]), b.dtype)
            _, hs = jax.lax.scan(step, h0, jnp.swapaxes(b, 0, 1))
            return jnp.swapaxes(hs, 0, 1)
        key = jax.random.key(seed)
        ks = jax.random.split(key, 10)
        s = 0.02
        return {'x': jax.random.normal(ks[0], (B, T, E), jnp.float32), 'tau_ctx': jnp.float32(_tau_init(max(T // 2, 4))), 'tau_raws': jnp.array([_tau_init(max(T // 2 ** i, 2)) for i in range(D)], jnp.float32), 'Wg': jax.random.normal(ks[1], (E, 2 * E), jnp.float32) * s, 'bg': jnp.full((E,), -0.5, jnp.float32), 'Wn1': jax.random.normal(ks[2], (E // 4, E), jnp.float32) * s, 'bn1': jnp.zeros((E // 4,), jnp.float32), 'Wn2': jax.random.normal(ks[3], (D, E // 4), jnp.float32) * s, 'bn2': jnp.zeros((D,), jnp.float32), 'blend': jax.random.normal(ks[4], (D, E), jnp.float32) * s, 'Wsoma': jax.random.normal(ks[5], (E, E), jnp.float32) * s, 'bsoma': jnp.zeros((E,), jnp.float32), 'Wtemp': jax.random.normal(ks[6], (E, E), jnp.float32) * s, 'btemp': jnp.zeros((E,), jnp.float32), 'Wout': jax.random.normal(ks[7], (E, E), jnp.float32) * s, 'gamma': jnp.ones((E,), jnp.float32), 'beta': jnp.zeros((E,), jnp.float32)}
    _L1_cond_all = _L1_cond_setup()
    _L1_cond_in = {k: v for k, v in _L1_cond_all.items() if k in ('tau_ctx', 'Wg', 'bg', 'Wn1', 'bn1', 'Wsoma', 'bsoma', 'Wtemp', 'btemp', 'Wout', 'gamma', 'beta')}
    del _L1_cond_all
    return {'x': x, 'itok_B_0_7': itok_B_0_7, 'condB_tauraws': condB_tauraws, 'cond_256': cond_256, 'condB_bn2': condB_bn2, 'cond_1024': cond_1024, 'L0_cond_weight': _L0_cond_in['weight'], 'L0_cond_bias': _L0_cond_in['bias'], 'L1_cond_tau_ctx': _L1_cond_in['tau_ctx'], 'L1_cond_Wg': _L1_cond_in['Wg'], 'L1_cond_bg': _L1_cond_in['bg'], 'L1_cond_Wn1': _L1_cond_in['Wn1'], 'L1_cond_bn1': _L1_cond_in['bn1'], 'L1_cond_Wsoma': _L1_cond_in['Wsoma'], 'L1_cond_bsoma': _L1_cond_in['bsoma'], 'L1_cond_Wtemp': _L1_cond_in['Wtemp'], 'L1_cond_btemp': _L1_cond_in['btemp'], 'L1_cond_Wout': _L1_cond_in['Wout'], 'L1_cond_gamma': _L1_cond_in['gamma'], 'L1_cond_beta': _L1_cond_in['beta']}

def reference(x, itok_B_0_7, condB_tauraws, cond_256, condB_bn2, cond_1024, L0_cond_weight, L0_cond_bias, L1_cond_tau_ctx, L1_cond_Wg, L1_cond_bg, L1_cond_Wn1, L1_cond_bn1, L1_cond_Wsoma, L1_cond_bsoma, L1_cond_Wtemp, L1_cond_btemp, L1_cond_Wout, L1_cond_gamma, L1_cond_beta):
    import jax
    import jax.numpy as jnp

    def _L0_cond_ref(x, subject_id, weight, bias):
        import jax, jax.numpy as jnp
        import numpy as np
        S, O, H = (8, 512, 512)
        B, N = (32, 256)
        W = weight[subject_id]
        b = bias[subject_id]
        y = jnp.einsum('bnh,boh->bno', x, W) + b[:, None, :]
        return y

    def _L1_cond_ref(x, tau_ctx, tau_raws, Wg, bg, Wn1, bn1, Wn2, bn2, blend, Wsoma, bsoma, Wtemp, btemp, Wout, gamma, beta):
        import jax, jax.numpy as jnp
        import numpy as np
        import math
        B, T, E, D = (4, 1024, 512, 4)

        def _tau_init(t):
            a = 0.1 ** (1.0 / max(t - 1, 1))
            tt = -math.log(max(a, 1e-10))
            return math.log(math.exp(tt) - 1 + 1e-10)

        def causal_ema(b, tau_raw):
            alpha = jnp.exp(-jax.nn.softplus(tau_raw)).astype(b.dtype)

            def step(h, bt):
                h = alpha * h + bt
                return (h, h)
            h0 = jnp.zeros((b.shape[0], b.shape[2]), b.dtype)
            _, hs = jax.lax.scan(step, h0, jnp.swapaxes(b, 0, 1))
            return jnp.swapaxes(hs, 0, 1)
        ctx = causal_ema(x, tau_ctx)
        gate_in = jnp.concatenate([x, ctx], axis=-1)
        wg = jax.nn.sigmoid(jnp.einsum('btc,ec->bte', gate_in, Wg) + bg)
        gated = x * wg
        h1 = jax.nn.gelu(jnp.einsum('btc,hc->bth', x, Wn1) + bn1, approximate=False)
        mod = 0.5 + jax.nn.sigmoid(jnp.einsum('bth,dh->btd', h1, Wn2) + bn2)
        traces = jax.vmap(lambda tau, m: causal_ema(gated * m[..., None], tau))(tau_raws, jnp.moveaxis(mod, -1, 0))
        blend_w = jax.nn.softmax(blend, axis=0)
        temporal = jnp.einsum('dbtc,dc->btc', traces, blend_w)
        gate = jax.nn.sigmoid(jnp.einsum('btc,ec->bte', temporal, Wtemp) + btemp)
        soma = jax.nn.gelu(jnp.einsum('btc,ec->bte', x, Wsoma) + bsoma, approximate=False)
        out = jnp.einsum('btc,ec->bte', soma * gate, Wout)
        mu = out.mean(-1, keepdims=True)
        var = out.var(-1, keepdims=True)
        return (out - mu) / jnp.sqrt(var + 1e-05) * gamma + beta
    x = x + _L0_cond_ref(x, itok_B_0_7, L0_cond_weight, L0_cond_bias)
    x = x + _L1_cond_ref(x, L1_cond_tau_ctx, condB_tauraws, L1_cond_Wg, L1_cond_bg, L1_cond_Wn1, L1_cond_bn1, cond_256, condB_bn2, cond_1024, L1_cond_Wsoma, L1_cond_bsoma, L1_cond_Wtemp, L1_cond_btemp, L1_cond_Wout, L1_cond_gamma, L1_cond_beta)
    return x

_drawn_inputs = setup_inputs


def setup_inputs(seed=0):
    import zlib

    import numpy as np

    out = dict(_drawn_inputs(seed))
    spreads = {'condB_bn2': (0.0, 2.0),
     'L1_cond_bg': (-0.5, 0.6),
     'L1_cond_bn1': (0.0, 0.8),
     'L1_cond_bsoma': (0.0, 0.1),
     'L1_cond_btemp': (0.0, 0.635),
     'L1_cond_gamma': (1.0, 0.2),
     'L1_cond_beta': (0.0, 0.1)}
    factors = {'condB_tauraws': 8.0, 'cond_256': 6.235, 'cond_1024': 8.0, 'L1_cond_Wn1': 6.571}
    for name, (base, spread) in spreads.items():
        noise = np.random.default_rng([zlib.crc32(name.encode()), seed]).standard_normal(out[name].shape)
        drawn = base * np.exp(spread * noise) if base else spread * noise
        out[name] = jnp.asarray(drawn.astype(out[name].dtype))
    for name, factor in factors.items():
        out[name] = (out[name] * factor).astype(out[name].dtype)
    return out
```

```python
from contextlib import ExitStack

import concourse.bass as bass
from concourse import mybir

P = 128
E = 512
KT = E // P
N = 512
D = 2
BATCH = 2
SEQ = 2048
TPB = SEQ // N
TILES = BATCH * TPB
HI, LO = 0, 1
EPS = 1e-5

ALU = mybir.AluOpType
ACT = mybir.ActivationFunctionType
F32 = mybir.dt.float32
F32R = mybir.dt.float32r

CTX_ORDER = (2, 3, 0, 1)

V_BG, V_BSOMA, V_BTEMP, V_BN1, V_BLEND = 0, 4, 8, 12, 13
V_COLS = 21
S_TAU_CTX, S_TAU, S_BN2, S_COLS = 0, 1, 3, 5


def build(nc, x_t, ids, w_subj, b_subj, w_g, w_n1, w_n2, w_soma, w_temp, w_out, vecs, scal, gamma, beta, out):
    out_v = out.rearrange("b (t j p) e -> (b t) j p e", p=P, j=KT)

    with ExitStack() as ctx:
        def sb(name, shape, dt=F32):
            return ctx.enter_context(nc.sbuf_tensor(name, shape, dt))

        def sem(name):
            return ctx.enter_context(nc.semaphore(name))

        wl0 = sb("wl0", [P, KT, 2, E], F32R)
        wg = sb("wg", [P, 2 * KT, 2, E], F32R)
        wn1 = sb("wn1", [P, 1, 2, E], F32R)
        wn2 = sb("wn2", [P, D, 2, P], F32R)
        wsoma = sb("wsoma", [P, KT, 2, E], F32R)
        wtemp = sb("wtemp", [P, KT, 2, E], F32R)
        wout = sb("wout", [P, KT, 2, E], F32R)
        xs_sgs = sb("xs_sgs", [P, KT, 2, N], F32R)
        ys = sb("ys", [P, KT, 2, N], F32R)
        cts = sb("cts", [P, KT + 2, 2, N], F32R)
        h1s = sb("h1s", [P, 2, N], F32R)
        xraw = sb("xraw", [P, KT, N])
        y = sb("y", [P, KT, N])
        soma = sb("soma", [P, KT, N])
        res = sb("res", [P, KT, E])
        th = sb("th", [P, 2, N])
        tr0 = sb("tr0", [P, 2, N])
        tr1 = sb("tr1", [P, N])
        h1 = sb("h1", [P, N])
        mod = sb("mod", [P, D, N])
        normed = sb("normed", [P, 2, E])
        ident = sb("ident", [P, P])
        gamma_b = sb("gamma_b", [P, E])
        beta_b = sb("beta_b", [P, E])
        vec = sb("vec", [P, V_COLS])
        half_b = sb("half_b", [P, V_BN1])
        bsubj = sb("bsubj", [P, BATCH, KT])
        w2raw = sb("w2raw", [P, D])
        w2hi = sb("w2hi", [P, D])
        sca = sb("sca", [P, S_COLS])
        half_bn2 = sb("half_bn2", [P, D])
        decay = sb("decay", [P, 1 + D])
        exps = sb("exps", [P, 1 + D])
        bmax = sb("bmax", [P, KT])
        bexp = sb("bexp", [P, D, KT])
        bsum = sb("bsum", [P, KT])
        blend = sb("blend", [P, D, KT])
        minus_half = sb("minus_half", [P, KT])
        eps = sb("eps", [P, KT])
        ctx_last = sb("ctx_last", [P, KT])
        tr_last = sb("tr_last", [P, D, KT])
        stats = sb("stats", [P, KT, 6])
        mv = sb("mv", [P, KT, 2])
        veps = sb("veps", [P, KT])
        rstd = sb("rstd", [P, KT])
        idt = sb("idt", [1, BATCH], mybir.dt.int32)

        psA = ctx.enter_context(nc.psum_tensor("psA", [P, KT, N], F32))
        psB = ctx.enter_context(nc.psum_tensor("psB", [P, KT, N], F32))

        ids_in, small_in = sem("ids_in"), sem("small_in")
        x_in = sem("x_in")
        w1_in = sem("w1_in")
        stored = sem("stored")
        SLOTS = 8
        stage_in = [sem(f"stage_in{s}") for s in range(SLOTS)]
        ident_zero, ident_done = sem("ident_zero"), sem("ident_done")
        diag_done = sem("diag_done")
        w_hi, w_lo = sem("w_hi"), sem("w_lo")
        w1_hi, w1_lo = sem("w1_hi"), sem("w1_lo")
        n2_hi, n2_done = sem("n2_hi"), sem("n2_done")
        setup = sem("setup")
        mh_done = sem("mh_done")
        exp_ready, exp_done = sem("exp_ready"), sem("exp_done")
        xh, xl = sem("xh"), sem("xl")
        l0_mm, g_mm, t_mm, s_mm, o_mm = (sem(f"{n}_mm") for n in ("l0", "g", "t", "s", "o"))
        n1_mm, mod_mm, yT_mm = sem("n1_mm"), sem("mod_mm"), sem("yT_mm")
        y_hi, y_lo = sem("y_hi"), sem("y_lo")
        ctx_raw, ctx_hi, ctx_lo, ctx_kept = (sem(f"ctx_{n}") for n in ("raw", "hi", "lo", "kept"))
        h1_hi, h1_lo = sem("h1_hi"), sem("h1_lo")
        mod_th, mod_done = sem("mod_th"), sem("mod_done")
        soma_done = sem("soma_done")
        g_th, gated = sem("g_th"), sem("gated")
        trace = sem("trace")
        blended, bl_hi, bl_lo = sem("blended"), sem("bl_hi"), sem("bl_lo")
        t_th, sg_raw, sg_hi, sg_lo = sem("t_th"), sem("sg_raw"), sem("sg_hi"), sem("sg_lo")
        res_copied, res_beta = sem("res_copied"), sem("res_beta")
        ln_stats, ln_mv, ln_centred, ln_eps, ln_rstd, result = (
            sem(f"ln_{n}") for n in ("stats", "mv", "centred", "eps", "rstd", "result"))

        def need(eng, semaphore, count):
            if not (isinstance(count, int) and count <= 0):
                eng.wait_ge(semaphore, count)

        def bits(ap):
            return ap.bitcast(F32)

        slices = ([("subj", k, wl0[:, k], 1.0) for k in range(KT)]
                  + [(w_n1, 0, wn1[:, 0], 1.0)]
                  + [(w_soma, k, wsoma[:, k], 1.0) for k in range(KT)]
                  + [(w_g, k, wg[:, k], 1.0) for k in range(2 * KT)]
                  + [(w_temp, k, wtemp[:, k], 1.0) for k in range(KT)]
                  + [(w_out, k, wout[:, k], 0.5) for k in range(KT)])
        AT_L0, AT_N1, AT_SOMA, AT_G, AT_TEMP, AT_OUT = 0, 4, 5, 9, 17, 21
        END = len(slices)
        stage = [res[:, 0], res[:, 1], res[:, 2], res[:, 3], th[:, 0], th[:, 1], normed[:, 0], normed[:, 1]]

        block = ctx.enter_context(nc.Block())

        def tr_slot(c):
            return KT + c if c < 2 else c - 2

        @block.sync
        def _(sp):
            sp.dma_start(idt[:], ids).then_inc(ids_in, 16)
            sp.dma_start(xraw[:], x_t[0]).then_inc(x_in, 16)
            sp.wait_ge(ids_in, 16)
            sid = [sp.value_load(idt[0:1, b:b + 1], min_val=0, max_val=w_subj.shape[0] - 1) for b in range(BATCH)]

            def subj(b, k):
                return w_subj[bass.ds(sid[b], 1), k].rearrange("s p e -> p (s e)")

            for i, (src, k, _, _) in enumerate(slices):
                if i >= SLOTS:
                    sp.wait_ge(w_lo, i - SLOTS + 1)
                sp.dma_start(stage[i % SLOTS], subj(0, k) if src == "subj" else src[k]).then_inc(stage_in[i % SLOTS], 16)
                if i == AT_N1:
                    for b in range(BATCH):
                        sp.dma_start(bsubj[:, b], b_subj[bass.ds(sid[b], 1)].rearrange("s p k -> p (s k)"))\
                          .then_inc(small_in, 16)

            def load_x(n):
                sp.wait_ge(xl, n * KT)
                sp.dma_start(xraw[:], x_t[bass.ds(n, 1)].rearrange("a p k t -> p (a k) t")).then_inc(x_in, 16)

            def store(n):
                for j in range(KT):
                    sp.wait_ge(result, n * KT + j + 1)
                    sp.dma_start(out_v[bass.ds(n, 1), j].rearrange("a p e -> p (a e)"), res[:, j]).then_inc(stored, 16)

            load_x(1)
            with sp.Fori(0, 2) as n:
                load_x(n + 2)
                store(n)
            sp.wait_ge(xl, 4 * KT)
            sp.dma_start(xraw[:], w_subj[bass.ds(sid[1], 1)].rearrange("s k p e -> p (s k) e")).then_inc(w1_in, 16)
            store(2)
            sp.wait_ge(w1_lo, KT)
            load_x(4)
            load_x(5)
            store(3)
            with sp.Fori(4, 6) as n:
                load_x(n + 2)
                store(n)
            store(6)
            store(7)
            sp.wait_ge(stored, TILES * KT * 16)

        @block.tensor
        def _(pe):
            def split_mm(dst, w, a, start, stop):
                pe.matmul(dst, w[HI], a[HI], start=start, stop=False)
                pe.matmul(dst, w[HI], a[LO], start=False, stop=False)
                return pe.matmul(dst, w[LO], a[HI], start=False, stop=stop)

            def cols(w, k, o):
                return [w[:, k, h, o * P:(o + 1) * P] for h in (HI, LO)]

            def pair(a, k):
                return [a[:, k, h] for h in (HI, LO)]

            def weights(count):
                pe.wait_ge(w_lo, count)

            def subject_layer(n, first=False):
                if not first:
                    need(pe, soma_done, n * KT)
                    need(pe, res_copied, n * KT)
                for k in range(KT):
                    if first:
                        weights(AT_L0 + k + 1)
                    need(pe, xl, n * KT + k + 1)
                    for o in range(KT):
                        m = split_mm(psB[:, o], cols(wl0, k, o), pair(xs_sgs, k), k == 0, k == KT - 1)
                        if k == KT - 1:
                            m.then_inc(l0_mm, 1)

            def hidden(n):
                for k in range(KT):
                    need(pe, y_lo, n * KT + k + 1)
                    m = split_mm(psB[:, 0], [wn1[:, 0, h, k * P:(k + 1) * P] for h in (HI, LO)], pair(ys, k),
                                 k == 0, k == KT - 1)
                m.then_inc(n1_mm, 1)

            def modulation(n):
                need(pe, h1_lo, n + 1)
                for d in range(D):
                    split_mm(psB[:, 2 + d], [wn2[:, d, h] for h in (HI, LO)], [h1s[:, h] for h in (HI, LO)],
                             True, True).then_inc(mod_mm, 1)

            def soma_layer(n, first=False):
                for o in range(KT):
                    if o >= 2:
                        need(pe, soma_done, n * KT + o - 1)
                    for k in range(KT):
                        if first and o == 0:
                            weights(AT_SOMA + k + 1)
                        m = split_mm(psB[:, o % 2], cols(wsoma, k, o), pair(ys, k), k == 0, k == KT - 1)
                    m.then_inc(s_mm, 1)

            def gate_layer(n, first=False):
                for o in range(KT):
                    if o == 0:
                        need(pe, ln_centred, n * KT)
                    for k in range(KT):
                        if first and o == 0:
                            weights(AT_G + k + 1)
                        split_mm(psA[:, o], cols(wg, k, o), pair(ys, k), k == 0, False)
                    for i, k in enumerate(CTX_ORDER):
                        if o == 0:
                            need(pe, ctx_lo, n * KT + i + 1)
                            if first:
                                weights(AT_G + 2 * KT)
                        m = split_mm(psA[:, o], cols(wg, KT + k, o), pair(cts, k), False, i == KT - 1)
                    m.then_inc(g_mm, 1)
                    if o < 2:
                        need(pe, mod_th, n * D + o + 1)
                    else:
                        need(pe, res_copied, n * KT + o - 1)
                    for k in range(KT):
                        m = pe.transpose(psB[:, 2 + o % 2, k * P:(k + 1) * P], y[:, k, o * P:(o + 1) * P], ident[:])
                    m.then_inc(yT_mm, 1)

            def temporal_layer(n, first=False):
                for k in range(KT):
                    if first:
                        weights(AT_TEMP + k + 1)
                    need(pe, bl_lo, n * KT + k + 1)
                    for o in range(KT):
                        if k == 0:
                            need(pe, g_th, n * KT + o + 1)
                        m = split_mm(psA[:, o], cols(wtemp, k, o), pair(cts, tr_slot(k)), k == 0, k == KT - 1)
                        if k == KT - 1:
                            m.then_inc(t_mm, 1)

            def output_layer(n, first=False):
                for k in range(KT):
                    if first:
                        weights(AT_OUT + k + 1)
                    need(pe, sg_lo, n * KT + k + 1)
                    for j in range(KT):
                        if k == 0:
                            need(pe, t_th, n * KT + j + 1)
                        m = split_mm(psA[:, j], [xs_sgs[:, k, h, j * P:(j + 1) * P] for h in (HI, LO)],
                                     pair(wout, k), k == 0, k == KT - 1)
                        if k == KT - 1:
                            m.then_inc(o_mm, 1)

            def step(n, first=False, last=False, boundary=False):
                gate_layer(n, first)
                if boundary:
                    pe.wait_ge(w1_lo, KT)
                if not last:
                    subject_layer(n + 1)
                temporal_layer(n, first)
                if not last:
                    hidden(n + 1)
                output_layer(n, first)
                if not last:
                    modulation(n + 1)
                    soma_layer(n + 1)

            subject_layer(0, first=True)
            weights(AT_N1 + 1)
            hidden(0)
            pe.wait_ge(n2_done, D)
            pe.wait_ge(ident_done, 1)
            modulation(0)
            soma_layer(0, first=True)
            step(0, first=True)
            with pe.Fori(1, 3) as n:
                step(n)
            step(3, boundary=True)
            with pe.Fori(4, TILES - 1) as n:
                step(n)
            step(TILES - 1, last=True)

        @block.scalar
        def _(act):
            act.dma_start(vec[:], vecs).then_inc(small_in, 16)
            act.dma_start(sca[:], scal.partition_broadcast(P)).then_inc(small_in, 16)
            act.dma_start(w2raw[:], w_n2).then_inc(small_in, 16)
            act.dma_start(gamma_b[:], gamma.partition_broadcast(P)).then_inc(small_in, 16)
            act.dma_start(beta_b[:], beta.partition_broadcast(P)).then_inc(small_in, 16)
            act.wait_ge(exp_ready, 1)
            act.activation(exps[:], sca[:, 0:1 + D], ACT.Exp).then_inc(exp_done, 1)
            act.activation(bexp[:], bexp[:], ACT.Exp).then_inc(exp_done, 1)

            def split_weight(i):
                if i < KT:
                    act.wait_ge(diag_done, i + 1)
                else:
                    act.wait_ge(stage_in[i % SLOTS], 16 * (i // SLOTS + 1))
                _, _, dst, scale = slices[i]
                act.activation(dst[:, HI], stage[i % SLOTS], ACT.Copy, scale=scale).then_inc(w_hi, 1)

            def split_x(n, first=False):
                need(act, x_in, (n + 1) * 16)
                if not first:
                    need(act, o_mm, (n - 1) * KT)
                for c in range(KT):
                    act.activation(xs_sgs[:, c, HI], xraw[:, c], ACT.Copy).then_inc(xh, 1)

            def make_y(n, b):
                need(act, gated, n * KT)
                need(act, yT_mm, n * KT)
                for o in range(KT):
                    need(act, l0_mm, n * KT + o + 1)
                    act.activation(y[:, o], psB[:, o], ACT.Identity, bias=bsubj[:, b, o:o + 1])
                    act.activation(ys[:, o, HI], psB[:, o], ACT.Identity, bias=bsubj[:, b, o:o + 1]).then_inc(y_hi, 1)

            def split_ctx(n, some):
                for i in some:
                    need(act, ctx_raw, n * KT + i + 1)
                    if i == 0:
                        need(act, g_mm, n * KT)
                    if i == 2:
                        need(act, t_mm, n * KT)
                    c = CTX_ORDER[i]
                    act.activation(cts[:, c, HI], tr0[:, c % 2], ACT.Copy).then_inc(ctx_hi, 1)

            def hidden(n):
                need(act, n1_mm, n + 1)
                need(act, h1_lo, n)
                need(act, mod_mm, n * D)
                act.activation(h1[:], psB[:, 0], ACT.Gelu, bias=vec[:, V_BN1:V_BN1 + 1])
                act.activation(h1s[:, HI], psB[:, 0], ACT.Gelu, bias=vec[:, V_BN1:V_BN1 + 1]).then_inc(h1_hi, 1)

            def modulation(n):
                need(act, blended, n * KT)
                for d in range(D):
                    need(act, mod_mm, n * D + d + 1)
                    act.activation(mod[:, d], psB[:, 2 + d], ACT.Tanh, bias=half_bn2[:, d:d + 1], scale=0.5)\
                       .then_inc(mod_th, 1)

            def soma_act(n):
                need(act, sg_raw, n * KT)
                for o in range(KT):
                    need(act, s_mm, n * KT + o + 1)
                    act.activation(soma[:, o], psB[:, o % 2], ACT.Gelu, bias=vec[:, V_BSOMA + o:V_BSOMA + o + 1])\
                       .then_inc(soma_done, 1)

            def split_blend(n, c):
                need(act, blended, n * KT + c + 1)
                if c == 0:
                    need(act, t_mm, n * KT)
                if c == 2:
                    need(act, g_mm, n * KT + KT)
                act.activation(cts[:, tr_slot(c), HI], tr0[:, c % 2], ACT.Copy).then_inc(bl_hi, 1)

            def gates(n, late_x=None):
                need(act, sg_lo, n * KT)
                need(act, stored, n * KT * 16)
                for o in range(KT):
                    need(act, g_mm, n * KT + o + 1)
                    if o >= 2:
                        need(act, blended, n * KT + o - 1)
                    act.activation(th[:, o % 2], psA[:, o], ACT.Tanh, bias=half_b[:, V_BG + o:V_BG + o + 1], scale=0.5)\
                       .then_inc(g_th, 1)
                    need(act, yT_mm, n * KT + o + 1)
                    act.activation(res[:, o], psB[:, 2 + o % 2], ACT.Copy).then_inc(res_copied, 1)
                    if o >= 1:
                        split_blend(n, o - 1)
                    if o == 2 and late_x is not None:
                        split_x(late_x)
                split_blend(n, KT - 1)

            def temporal_gates(n, last=False):
                for i in range(KT + 1):
                    if i < KT:
                        need(act, t_mm, n * KT + i + 1)
                        if i < 2:
                            need(act, blended, n * KT + i + 3)
                        else:
                            need(act, sg_lo, n * KT + i - 1)
                        act.activation(th[:, i % 2], psA[:, i], ACT.Tanh,
                                       bias=half_b[:, V_BTEMP + i:V_BTEMP + i + 1], scale=0.5).then_inc(t_th, 1)
                    if i >= 1:
                        need(act, sg_raw, n * KT + i)
                        act.activation(xs_sgs[:, i - 1, HI], th[:, (i - 1) % 2], ACT.Copy).then_inc(sg_hi, 1)

            def step(n, b_next, last=False, boundary=False):
                if boundary:
                    for k in range(KT):
                        act.wait_ge(diag_done, KT + k + 1)
                        if k == 0:
                            need(act, l0_mm, n * KT + KT)
                        act.activation(wl0[:, k, HI], xraw[:, k], ACT.Copy).then_inc(w1_hi, 1)
                    gates(n, late_x=n + 1)
                else:
                    if not last:
                        split_x(n + 1)
                    gates(n)
                if not last:
                    make_y(n + 1, b_next)
                    split_ctx(n + 1, (0, 1))
                temporal_gates(n)
                if not last:
                    hidden(n + 1)
                    split_ctx(n + 1, (2, 3))
                    modulation(n + 1)
                    soma_act(n + 1)

            split_x(0, first=True)
            for i in range(AT_G):
                split_weight(i)
            act.wait_ge(small_in, 16 * 7)
            make_y(0, 0)
            for i in range(AT_G, AT_G + KT):
                split_weight(i)
            hidden(0)
            split_ctx(0, (0, 1))
            for i in range(AT_G + KT, AT_TEMP):
                split_weight(i)
            split_ctx(0, (2, 3))
            act.wait_ge(setup, 1)
            modulation(0)
            soma_act(0)
            for i in range(AT_TEMP, END):
                split_weight(i)
            act.wait_ge(w_lo, END)
            step(0, 0)
            with act.Fori(1, 3) as n:
                step(n, 0)
            step(3, 1, boundary=True)
            with act.Fori(4, TILES - 1) as n:
                step(n, 1)
            step(TILES - 1, 1, last=True)

        @block.gpsimd
        def _(pool):
            def split_x(n):
                for c in range(KT):
                    need(pool, xh, n * KT + c + 1)
                    pool.tensor_tensor(xs_sgs[:, c, LO], xraw[:, c], bits(xs_sgs[:, c, HI]), ALU.subtract).then_inc(xl, 1)

            def add_beta(n):
                for j in range(KT):
                    need(pool, res_copied, n * KT + j + 1)
                    pool.tensor_tensor(res[:, j], res[:, j], beta_b[:], ALU.add).then_inc(res_beta, 1)

            def inv_std(n):
                need(pool, ln_mv, n * KT + KT)
                need(pool, result, n * KT)
                pool.tensor_tensor(veps[:], mv[:, :, 1], eps[:], ALU.add).then_inc(ln_eps, 1)
                need(pool, ln_eps, n + 1)
                pool.tensor_tensor(rstd[:], veps[:], minus_half[:], ALU.pow).then_inc(ln_rstd, 1)

            pool.memset(ident[:], 0.0).then_inc(ident_zero, 1)
            pool.wait_ge(ident_zero, 1)
            pool.affine_select(out=ident[:], in_=ident[:], compare_op=ALU.not_equal, fill=1.0, base=0,
                               pattern=[[-1, P]], channel_multiplier=1).then_inc(ident_done, 1)
            pool.memset(eps[:], EPS)
            pool.memset(minus_half[:], -0.5).then_inc(mh_done, 1)
            split_x(0)
            pool.wait_ge(small_in, 16 * 7)
            pool.wait_ge(mh_done, 1)

            def step(n, last=False):
                if not last:
                    split_x(n + 1)
                add_beta(n)
                inv_std(n)

            step(0)
            with pool.Fori(1, 3) as n:
                step(n)
            add_two = 3 * KT
            for j in range(2):
                pool.wait_ge(res_copied, add_two + j + 1)
                pool.tensor_tensor(res[:, j], res[:, j], beta_b[:], ALU.add).then_inc(res_beta, 1)
            split_x(4)
            for j in range(2, KT):
                pool.wait_ge(res_copied, add_two + j + 1)
                pool.tensor_tensor(res[:, j], res[:, j], beta_b[:], ALU.add).then_inc(res_beta, 1)
            inv_std(3)
            with pool.Fori(4, TILES - 1) as n:
                step(n)
            step(TILES - 1, last=True)

        @block.vector
        def _(dve):
            def stt(dst, a, s, b, op0, op1):
                return dve.scalar_tensor_tensor(out=dst, in0=a, scalar=s, in1=b, op0=op0, op1=op1)

            def minus(dst, a, hi):
                return dve.tensor_tensor(dst, a, bits(hi), ALU.subtract)

            links = [0]
            const = sem("const")

            def link(ins):
                links[0] += 1
                ins.then_inc(const, 1)
                dve.wait_ge(const, links[0])

            dve.memset(ctx_last[:], 0.0)
            link(dve.memset(tr_last[:], 0.0))
            dve.wait_ge(small_in, 16 * 7)
            bl = [vec[:, V_BLEND + d * KT:V_BLEND + (d + 1) * KT] for d in range(D)]
            link(dve.tensor_tensor(bmax[:], bl[0], bl[1], ALU.max))
            for d in range(D):
                m = dve.tensor_tensor(bexp[:, d], bl[d], bmax[:], ALU.subtract)
            m.then_inc(exp_ready, 1)
            dve.tensor_scalar(half_bn2[:], sca[:, S_BN2:S_BN2 + D], 0.5, None, ALU.mult)
            dve.tensor_scalar(half_b[:], vec[:, 0:V_BN1], 0.5, None, ALU.mult).then_inc(setup, 1)
            for d in range(D):
                dve.tensor_copy(wn2[:, d, HI], w2raw[:, d:d + 1].to_broadcast([P, P])).then_inc(n2_hi, 1)
            dve.wait_ge(n2_hi, D)
            for d in range(D):
                minus(wn2[:, d, LO], w2raw[:, d:d + 1].to_broadcast([P, P]), wn2[:, d, HI]).then_inc(n2_done, 1)
            dve.wait_ge(exp_done, 2)
            link(dve.tensor_scalar(exps[:], exps[:], 1.0, None, ALU.add))
            link(dve.reciprocal(decay[:], exps[:]))
            link(dve.tensor_tensor(bsum[:], bexp[:, 0], bexp[:, 1], ALU.add))
            link(dve.reciprocal(bsum[:], bsum[:]))
            for d in range(D):
                link(stt(blend[:, d], bexp[:, d], 0.25, bsum[:], ALU.mult, ALU.mult))

            def add_identity(buf, k, count):
                block_k = buf[:, k * P:(k + 1) * P]
                dve.tensor_tensor(block_k, block_k, ident[:], ALU.add).then_inc(diag_done, 1)

            def split_weight(i):
                _, _, dst, scale = slices[i]
                if i < KT:
                    dve.wait_ge(stage_in[i], 16)
                    add_identity(stage[i], i, i)
                dve.wait_ge(w_hi, i + 1)
                if scale == 1.0:
                    minus(dst[:, LO], stage[i % SLOTS], dst[:, HI]).then_inc(w_lo, 1)
                else:
                    stt(dst[:, LO], stage[i % SLOTS], scale, bits(dst[:, HI]), ALU.mult, ALU.subtract).then_inc(w_lo, 1)

            def y_low(n):
                for o in range(KT):
                    need(dve, y_hi, n * KT + o + 1)
                    minus(ys[:, o, LO], y[:, o], ys[:, o, HI]).then_inc(y_lo, 1)

            def context(n, some):
                if 0 in some:
                    need(dve, ctx_kept, n * KT)
                    need(dve, bl_lo, n * KT)
                else:
                    need(dve, ctx_lo, n * KT + 2)
                for i in some:
                    c = CTX_ORDER[i]
                    dve.tensor_tensor_scan(tr0[:, c % 2], decay[:, 0:1].to_broadcast([P, N]), y[:, c],
                                           ctx_last[:, c:c + 1], ALU.mult, ALU.add).then_inc(ctx_raw, 1)
                for i in some:
                    c = CTX_ORDER[i]
                    need(dve, ctx_raw, n * KT + i + 1)
                    dve.tensor_copy(ctx_last[:, c:c + 1], tr0[:, c % 2, N - 1:N]).then_inc(ctx_kept, 1)
                    need(dve, ctx_hi, n * KT + i + 1)
                    minus(cts[:, c, LO], tr0[:, c % 2], cts[:, c, HI]).then_inc(ctx_lo, 1)

            def hidden(n):
                need(dve, h1_hi, n + 1)
                minus(h1s[:, LO], h1[:], h1s[:, HI]).then_inc(h1_lo, 1)

            def modulation(n):
                for d in range(D):
                    need(dve, mod_th, n * D + d + 1)
                    dve.tensor_scalar(mod[:, d], mod[:, d], 2.0, None, ALU.add).then_inc(mod_done, 1)

            def blend_low(n, c):
                need(dve, bl_hi, n * KT + c + 1)
                minus(cts[:, tr_slot(c), LO], tr0[:, c % 2], cts[:, tr_slot(c), HI]).then_inc(bl_lo, 1)

            def traces(n):
                STEPS = 6
                need(dve, mod_done, n * D + D)
                need(dve, trace, n * KT * STEPS)
                need(dve, blended, n * KT)
                need(dve, ctx_lo, n * KT + KT)
                for c in range(KT):
                    s = c % 2
                    base = n * KT * STEPS + c * STEPS
                    need(dve, g_th, n * KT + c + 1)
                    if c >= 1:
                        need(dve, blended, n * KT + c)
                    stt(th[:, s], th[:, s], 1.0, y[:, c], ALU.add, ALU.mult).then_inc(gated, 1)
                    need(dve, gated, n * KT + c + 1)
                    if c >= 2:
                        need(dve, bl_lo, n * KT + c - 1)
                    stt(tr0[:, s], th[:, s], blend[:, 0, c:c + 1], mod[:, 0], ALU.mult, ALU.mult).then_inc(trace, 1)
                    stt(tr1[:], th[:, s], blend[:, 1, c:c + 1], mod[:, 1], ALU.mult, ALU.mult).then_inc(trace, 1)
                    if c >= 1:
                        blend_low(n, c - 1)
                    for d, buf in enumerate((tr0[:, s], tr1[:])):
                        dve.wait_ge(trace, base + d + 1)
                        dve.tensor_tensor_scan(buf, decay[:, 1 + d:2 + d].to_broadcast([P, N]), buf,
                                               tr_last[:, d, c:c + 1], ALU.mult, ALU.add).then_inc(trace, 1)
                    for d, buf in enumerate((tr0[:, s], tr1[:])):
                        dve.wait_ge(trace, base + D + d + 1)
                        dve.tensor_copy(tr_last[:, d, c:c + 1], buf[:, N - 1:N]).then_inc(trace, 1)
                    dve.wait_ge(trace, base + D + D + 1)
                    dve.tensor_tensor(tr0[:, s], tr0[:, s], tr1[:], ALU.add).then_inc(blended, 1)
                    if c == 0 and hooks:
                        hooks.pop()()
                blend_low(n, KT - 1)

            def soma_gate(n):
                need(dve, soma_done, n * KT + KT)
                for c in range(KT + 1):
                    if c < KT:
                        need(dve, t_th, n * KT + c + 1)
                        stt(th[:, c % 2], th[:, c % 2], 1.0, soma[:, c], ALU.add, ALU.mult).then_inc(sg_raw, 1)
                    if c >= 1:
                        need(dve, sg_hi, n * KT + c)
                        minus(xs_sgs[:, c - 1, LO], th[:, (c - 1) % 2], xs_sgs[:, c - 1, HI]).then_inc(sg_lo, 1)

            def norm(n):
                def stats_of(j):
                    need(dve, o_mm, n * KT + j + 1)
                    dve.bn_stats(stats[:, j], psA[:, j]).then_inc(ln_stats, 1)

                def aggregate(j):
                    dve.bn_aggr(mv[:, j], stats[:, j]).then_inc(ln_mv, 1)

                def centre(j):
                    need(dve, ln_mv, n * KT + j + 1)
                    stt(normed[:, j % 2], psA[:, j], mv[:, j, 0:1], gamma_b[:], ALU.subtract, ALU.mult)\
                        .then_inc(ln_centred, 1)

                def finish(j):
                    need(dve, ln_centred, n * KT + j + 1)
                    need(dve, res_beta, n * KT + j + 1)
                    stt(res[:, j], normed[:, j % 2], rstd[:, j:j + 1], res[:, j], ALU.mult, ALU.add)\
                        .then_inc(result, 1)

                need(dve, ln_rstd, n)
                need(dve, result, n * KT)
                stats_of(0)
                for j in range(1, KT):
                    need(dve, ln_stats, n * KT + j)
                    stats_of(j)
                    aggregate(j - 1)
                need(dve, ln_stats, n * KT + KT)
                centre(0)
                aggregate(KT - 1)
                centre(1)
                need(dve, ln_rstd, n + 1)
                for j in range(KT):
                    finish(j)
                    if j + 2 < KT:
                        need(dve, result, n * KT + j + 1)
                        centre(j + 2)

            hooks = []

            def step(n, last=False):
                traces(n)
                if not last:
                    y_low(n + 1)
                    context(n + 1, (0, 1))
                soma_gate(n)
                if not last:
                    hidden(n + 1)
                    context(n + 1, (2, 3))
                norm(n)
                if not last:
                    modulation(n + 1)

            dve.wait_ge(ident_done, 1)
            for i in range(AT_G):
                split_weight(i)
            y_low(0)
            for i in range(AT_G, AT_G + KT):
                split_weight(i)
            hidden(0)
            context(0, (0, 1))
            for i in range(AT_G + KT, AT_TEMP):
                split_weight(i)
            context(0, (2, 3))
            modulation(0)
            for i in range(AT_TEMP, END):
                split_weight(i)
            dve.wait_ge(w_lo, END)
            step(0)
            with dve.Fori(1, 3) as n:
                step(n)
            dve.wait_ge(w1_in, 16)
            for k in range(KT):
                add_identity(xraw[:, k], k, KT + k)

            def second_weights_low():
                for k in range(KT):
                    dve.wait_ge(w1_hi, k + 1)
                    minus(wl0[:, k, LO], xraw[:, k], wl0[:, k, HI]).then_inc(w1_lo, 1)
                dve.wait_ge(ctx_kept, TPB * KT)
                link(dve.memset(ctx_last[:], 0.0))

            hooks.append(second_weights_low)
            step(3)
            dve.wait_ge(trace, TPB * KT * 6)
            link(dve.memset(tr_last[:], 0.0))
            with dve.Fori(4, TILES - 1) as n:
                step(n)
            step(TILES - 1, last=True)


def kernel(x, itok_B_0_7, condB_tauraws, cond_256, condB_bn2, cond_1024, L0_cond_weight, L0_cond_bias,
           L1_cond_tau_ctx, L1_cond_Wg, L1_cond_bg, L1_cond_Wn1, L1_cond_bn1, L1_cond_Wsoma, L1_cond_bsoma,
           L1_cond_Wtemp, L1_cond_btemp, L1_cond_Wout, L1_cond_gamma, L1_cond_beta):
    import numpy as np
    import concourse.bacc as bacc
    from concourse.bass_utils import run_bass_kernel_spmd

    def rows(w):
        w = np.asarray(w)
        return np.ascontiguousarray(w.T.reshape(-1, P, w.shape[0]))

    def chan(v):
        return np.asarray(v).reshape(-1, P).T

    subj = np.asarray(L0_cond_weight)
    arrays = {
        "x_t": np.ascontiguousarray(np.asarray(x).reshape(TILES, N, KT, P).transpose(0, 3, 2, 1)),
        "ids": np.asarray(itok_B_0_7).reshape(1, BATCH),
        "w_subj": np.ascontiguousarray(subj.transpose(0, 2, 1).reshape(subj.shape[0], KT, P, E)),
        "b_subj": np.ascontiguousarray(np.asarray(L0_cond_bias).reshape(-1, KT, P).transpose(0, 2, 1)),
        "w_g": rows(L1_cond_Wg),
        "w_n1": np.ascontiguousarray(rows(L1_cond_Wn1).transpose(1, 0, 2).reshape(1, P, E)),
        "w_n2": np.ascontiguousarray(np.asarray(cond_256).T),
        "w_soma": rows(L1_cond_Wsoma),
        "w_temp": rows(L1_cond_Wtemp),
        "w_out": rows(L1_cond_Wout),
        "vecs": np.ascontiguousarray(np.concatenate(
            [chan(L1_cond_bg), chan(L1_cond_bsoma), chan(L1_cond_btemp), chan(L1_cond_bn1),
             *[chan(row) for row in np.asarray(cond_1024)]], axis=1)),
        "scal": np.concatenate([np.asarray(L1_cond_tau_ctx).reshape(1), np.asarray(condB_tauraws),
                                np.asarray(condB_bn2)]),
        "gamma": np.asarray(L1_cond_gamma),
        "beta": np.asarray(L1_cond_beta),
    }
    nc = bacc.Bacc("TRN2", target_bir_lowering=False, num_devices=1, dynamic_dma_scratch_size=1024)
    aps = {k: nc.dram_tensor(f"in_{k}", a.shape, mybir.dt.from_np(a.dtype), kind="ExternalInput").ap()
           for k, a in arrays.items()}
    out = nc.dram_tensor("out_0", (BATCH, SEQ, E), F32, kind="ExternalOutput").ap()
    build(nc, **aps, out=out)
    r = run_bass_kernel_spmd(nc, [{f"in_{k}": a for k, a in arrays.items()}], core_ids=[0])
    return r.results[0]["out_0"]
```

```python
from contextlib import ExitStack

import concourse.bass as bass
from concourse import mybir

P = 128
E = 512
KT = E // P
N = 512
D = 2
BATCH = 2
SEQ = 2048
TPB = SEQ // N
TILES = BATCH * TPB
HI, LO = 0, 1
EPS = 1e-5

ALU = mybir.AluOpType
ACT = mybir.ActivationFunctionType
F32 = mybir.dt.float32
F32R = mybir.dt.float32r

CTX_ORDER = (2, 3, 0, 1)

V_BG, V_BSOMA, V_BTEMP, V_BN1, V_BLEND = 0, 4, 8, 12, 13
V_COLS = 21
S_COLS = 1 + D


def build(nc, x_t, ids, w_subj, b_subj, w_g, w_n1, w_n2, w_soma, w_temp, w_out, vecs, scal, bn_2, gamma, beta, out):
    mod_dram = nc.dram_tensor("mod_rows", (D * N,), F32).ap()
    out_v = out.rearrange("b (t j p) e -> (b t) j p e", p=P, j=KT)

    with ExitStack() as ctx:
        def sb(name, shape, dt=F32):
            return ctx.enter_context(nc.sbuf_tensor(name, shape, dt))

        def sem(name):
            return ctx.enter_context(nc.semaphore(name))

        wl0 = sb("wl0", [P, KT, 2, E], F32R)
        wg = sb("wg", [P, 2 * KT, 2, E], F32R)
        wn1 = sb("wn1", [P, 1, 2, E], F32R)
        wn2 = sb("wn2", [P, 2, P], F32R)
        wsoma = sb("wsoma", [P, KT, 2, E], F32R)
        wtemp = sb("wtemp", [P, KT, 2, E], F32R)
        wout = sb("wout", [P, KT, 2, E], F32R)
        xs_sgs = sb("xs_sgs", [P, KT, 2, N], F32R)
        ys = sb("ys", [P, KT, 2, N], F32R)
        cts = sb("cts", [P, KT + 2, 2, N], F32R)
        h1s = sb("h1s", [P, 2, N], F32R)
        xraw = sb("xraw", [P, KT, N])
        y = sb("y", [P, KT, N])
        soma = sb("soma", [P, KT, N])
        res = sb("res", [P, KT, E])
        th = sb("th", [P, 2, N])
        tr0 = sb("tr0", [P, 2, N])
        tr1 = sb("tr1", [P, N])
        h1 = sb("h1", [P, N])
        mod_row = sb("mod_row", [D, N])
        mod = sb("mod", [P, D, N])
        normed = sb("normed", [P, 2, E])
        ident = sb("ident", [P, P])
        gamma_b = sb("gamma_b", [P, E])
        beta_b = sb("beta_b", [P, E])
        vec = sb("vec", [P, V_COLS])
        half_b = sb("half_b", [P, V_BN1])
        bsubj = sb("bsubj", [P, BATCH, KT])
        w2raw = sb("w2raw", [P, D])
        w2wide = sb("w2wide", [P, P])
        unused = sb("unused", [P, 1])
        sca = sb("sca", [P, S_COLS])
        bn2 = sb("bn2", [D, 1])
        half_bn2 = sb("half_bn2", [D, 1])
        decay = sb("decay", [P, 1 + D])
        exps = sb("exps", [P, 1 + D])
        bmax = sb("bmax", [P, KT])
        bexp = sb("bexp", [P, D, KT])
        bsum = sb("bsum", [P, KT])
        blend = sb("blend", [P, D, KT])
        minus_half = sb("minus_half", [P, 1])
        eps = sb("eps", [P, 1])
        ctx_last = sb("ctx_last", [P, KT])
        tr_last = sb("tr_last", [P, D, KT])
        stats = sb("stats", [P, KT, 6])
        mv = sb("mv", [P, KT, 2])
        veps = sb("veps", [P, KT])
        rstd = sb("rstd", [P, KT])
        idt = sb("idt", [1, BATCH], mybir.dt.int32)

        psA = ctx.enter_context(nc.psum_tensor("psA", [P, KT, N], F32))
        psB = ctx.enter_context(nc.psum_tensor("psB", [P, KT, N], F32))

        ids_in, small_in, bsubj_in, affine_in = (sem(f"{n}_in") for n in ("ids", "small", "bsubj", "affine"))
        x0_in = [sem(f"x0_in{c}") for c in range(KT)]
        x_in = sem("x_in")
        w1_in = sem("w1_in")
        stored = sem("stored")
        SLOTS = 8
        stage_in = [sem(f"stage_in{s}") for s in range(SLOTS)]
        ident_zero, ident_done = sem("ident_zero"), sem("ident_done")
        diag_done = sem("diag_done")
        w_hi, w_lo = sem("w_hi"), sem("w_lo")
        w1_hi, w1_lo = sem("w1_hi"), sem("w1_lo")
        n2_hi, n2_done = sem("n2_hi"), sem("n2_done")
        setup = sem("setup")
        mh_done = sem("mh_done")
        exp_ready, exp_done = sem("exp_ready"), sem("exp_done")
        xh, xl = sem("xh"), sem("xl")
        l0_mm, g_mm, t_mm, s_mm, o_mm = (sem(f"{n}_mm") for n in ("l0", "g", "t", "s", "o"))
        n1_mm, mod_mm, yT_mm = sem("n1_mm"), sem("mod_mm"), sem("yT_mm")
        y_hi, y_lo = sem("y_hi"), sem("y_lo")
        ctx_raw, ctx_hi, ctx_lo, ctx_kept = (sem(f"ctx_{n}") for n in ("raw", "hi", "lo", "kept"))
        h1_hi, h1_lo = sem("h1_hi"), sem("h1_lo")
        mod_th, mod_two = sem("mod_th"), sem("mod_two")
        mod_sent, mod_done = sem("mod_sent"), sem("mod_done")
        soma_done = sem("soma_done")
        g_th, gated = sem("g_th"), sem("gated")
        trace = sem("trace")
        blended, bl_hi, bl_lo = sem("blended"), sem("bl_hi"), sem("bl_lo")
        t_th, sg_raw, sg_hi, sg_lo = sem("t_th"), sem("sg_raw"), sem("sg_hi"), sem("sg_lo")
        res_copied, res_beta = sem("res_copied"), sem("res_beta")
        ln_stats, ln_mv, ln_centred, ln_eps, ln_rstd, result = (
            sem(f"ln_{n}") for n in ("stats", "mv", "centred", "eps", "rstd", "result"))

        def need(eng, semaphore, count):
            if not (isinstance(count, int) and count <= 0):
                eng.wait_ge(semaphore, count)

        def bits(ap):
            return ap.bitcast(F32)

        slices = ([("subj", k, wl0[:, k], 1.0) for k in range(KT)]
                  + [(w_n1, 0, wn1[:, 0], 1.0)]
                  + [(w_soma, k, wsoma[:, k], 1.0) for k in range(KT)]
                  + [(w_g, k, wg[:, k], 1.0) for k in range(2 * KT)]
                  + [(w_temp, k, wtemp[:, k], 1.0) for k in range(KT)]
                  + [(w_out, k, wout[:, k], 0.5) for k in range(KT)])
        AT_L0, AT_N1, AT_SOMA, AT_G, AT_TEMP, AT_OUT = 0, 4, 5, 9, 17, 21
        END = len(slices)
        stage = [res[:, 0], res[:, 1], res[:, 2], res[:, 3], th[:, 0], th[:, 1], normed[:, 0], normed[:, 1]]

        block = ctx.enter_context(nc.Block())

        gate_slots = [th[:, 0], th[:, 1], normed[:, 0], normed[:, 1]]

        def tr_slot(c):
            return KT + c if c < 2 else c - 2

        @block.sync
        def _(sp):
            sp.dma_start(idt[:], ids).then_inc(ids_in, 16)

            def load_x0(c):
                sp.dma_start(xraw[:, c], x_t[0, :, c]).then_inc(x0_in[c], 16)

            load_x0(0)
            sp.wait_ge(ids_in, 16)
            sid = [sp.value_load(idt[0:1, b:b + 1], min_val=0, max_val=w_subj.shape[0] - 1) for b in range(BATCH)]
            for i, (src, k, _, _) in enumerate(slices):
                if i >= SLOTS:
                    sp.wait_ge(w_lo, i - SLOTS + 1)
                rows_k = w_subj[bass.ds(sid[0], 1), k].rearrange("s p e -> p (s e)") if src == "subj" else src[k]
                sp.dma_start(stage[i % SLOTS], rows_k).then_inc(stage_in[i % SLOTS], 16)
                if i + 1 < KT:
                    load_x0(i + 1)
                if i == AT_N1:
                    for b in range(BATCH):
                        sp.dma_start(bsubj[:, b], b_subj[bass.ds(sid[b], 1)].rearrange("s p k -> p (s k)"))\
                          .then_inc(bsubj_in, 16)
            sp.dma_start(gamma_b[:], gamma.partition_broadcast(P)).then_inc(affine_in, 16)
            sp.dma_start(beta_b[:], beta.partition_broadcast(P)).then_inc(affine_in, 16)

            def load_x(n):
                sp.wait_ge(xl, n * KT)
                sp.dma_start(xraw[:], x_t[bass.ds(n, 1)].rearrange("a p k t -> p (a k) t")).then_inc(x_in, 16)

            def store(n):
                for j in range(KT):
                    sp.wait_ge(result, n * KT + j + 1)
                    sp.dma_start(out_v[bass.ds(n, 1), j].rearrange("a p e -> p (a e)"), res[:, j]).then_inc(stored, 16)

            def spread_mod(n):
                need(sp, mod_two, n + 1)
                sp.dma_start(mod_dram.rearrange("(d n) -> d n", d=D), mod_row[:]).then_inc(mod_sent, 16)
                need(sp, mod_sent, (n + 1) * 16)
                need(sp, blended, n * KT)
                sp.dma_start(mod[:].rearrange("p d n -> p (d n)"), mod_dram.partition_broadcast(P)).then_inc(mod_done, 16)

            load_x(1)
            spread_mod(0)
            with sp.Fori(0, 2) as n:
                load_x(n + 2)
                store(n)
                spread_mod(n + 1)
            sp.wait_ge(xl, 4 * KT)
            sp.dma_start(xraw[:], w_subj[bass.ds(sid[1], 1)].rearrange("s k p e -> p (s k) e")).then_inc(w1_in, 16)
            store(2)
            spread_mod(3)
            sp.wait_ge(w1_lo, KT)
            load_x(4)
            load_x(5)
            store(3)
            spread_mod(4)
            with sp.Fori(4, 6) as n:
                load_x(n + 2)
                store(n)
                spread_mod(n + 1)
            store(6)
            spread_mod(7)
            store(7)
            sp.wait_ge(stored, TILES * KT * 16)

        @block.tensor
        def _(pe):
            def split_mm(dst, w, a, start, stop):
                pe.matmul(dst, w[HI], a[HI], start=start, stop=False)
                pe.matmul(dst, w[HI], a[LO], start=False, stop=False)
                return pe.matmul(dst, w[LO], a[HI], start=False, stop=stop)

            def cols(w, k, o):
                return [w[:, k, h, o * P:(o + 1) * P] for h in (HI, LO)]

            def pair(a, k):
                return [a[:, k, h] for h in (HI, LO)]

            def weights(count):
                pe.wait_ge(w_lo, count)

            def subject_layer(n, first=False):
                if not first:
                    need(pe, soma_done, n * KT)
                for k in range(KT):
                    if first:
                        weights(AT_L0 + k + 1)
                    need(pe, xl, n * KT + k + 1)
                    for o in range(KT):
                        if k == 0 and o >= 2 and not first:
                            need(pe, res_copied, n * KT + o - 3)
                        m = split_mm(psB[:, o], cols(wl0, k, o), pair(xs_sgs, k), k == 0, k == KT - 1)
                        if k == KT - 1:
                            m.then_inc(l0_mm, 1)

            def hidden(n):
                for k in range(KT):
                    need(pe, y_lo, n * KT + k + 1)
                    m = split_mm(psB[:, 0], [wn1[:, 0, h, k * P:(k + 1) * P] for h in (HI, LO)], pair(ys, k),
                                 k == 0, k == KT - 1)
                m.then_inc(n1_mm, 1)

            def modulation(n):
                need(pe, h1_lo, n + 1)
                split_mm(psB[:, 2], [wn2[:, h] for h in (HI, LO)], [h1s[:, h] for h in (HI, LO)],
                         True, True).then_inc(mod_mm, 1)

            def soma_layer(n, first=False):
                for o in range(KT):
                    if o == 1:
                        need(pe, h1_hi, n + 1)
                    if o >= 2:
                        need(pe, soma_done, n * KT + o - 1)
                    for k in range(KT):
                        if first and o == 0:
                            weights(AT_SOMA + k + 1)
                        m = split_mm(psB[:, 1 - o % 2], cols(wsoma, k, o), pair(ys, k), k == 0, k == KT - 1)
                    m.then_inc(s_mm, 1)

            def transpose_y(n, j, bank):
                for k in range(KT):
                    m = pe.transpose(psB[:, bank, k * P:(k + 1) * P], y[:, k, j * P:(j + 1) * P], ident[:])
                m.then_inc(yT_mm, 1)

            def gate_layer(n, first=False, last=False):
                for o in range(KT):
                    if o == 0:
                        need(pe, ln_centred, n * KT)
                    for k in range(KT):
                        if first and o == 0:
                            weights(AT_G + k + 1)
                        split_mm(psA[:, o], cols(wg, k, o), pair(ys, k), k == 0, False)
                    for i, k in enumerate(CTX_ORDER):
                        if o == 0:
                            need(pe, ctx_lo, n * KT + i + 1)
                            if first:
                                weights(AT_G + 2 * KT)
                        m = split_mm(psA[:, o], cols(wg, KT + k, o), pair(cts, k), False, i == KT - 1)
                    m.then_inc(g_mm, 1)
                    if not last:
                        if o == 0:
                            need(pe, mod_th, n + 1)
                        if o >= 2:
                            need(pe, res_copied, n * KT + o - 1)
                        transpose_y(n, o, 2 + o % 2)

            def temporal_layer(n, first=False):
                for k in range(KT):
                    if first:
                        weights(AT_TEMP + k + 1)
                    need(pe, bl_lo, n * KT + k + 1)
                    for o in range(KT):
                        if k == 0:
                            need(pe, g_th, n * KT + o + 1)
                        m = split_mm(psA[:, o], cols(wtemp, k, o), pair(cts, tr_slot(k)), k == 0, k == KT - 1)
                        if k == KT - 1:
                            m.then_inc(t_mm, 1)

            def output_layer(n, whole_k):
                def product(k, j):
                    return split_mm(psA[:, j], [xs_sgs[:, k, h, j * P:(j + 1) * P] for h in (HI, LO)],
                                    pair(wout, k), k == 0, k == KT - 1)

                for k in range(whole_k):
                    need(pe, sg_lo, n * KT + k + 1)
                    for j in range(KT):
                        if k == 0:
                            need(pe, t_th, n * KT + j + 1)
                        product(k, j)
                need(pe, sg_lo, n * KT + KT)
                for j in range(KT):
                    for k in range(whole_k, KT):
                        m = product(k, j)
                    m.then_inc(o_mm, 1)

            def step(n, first=False, last=False, boundary=False):
                gate_layer(n, first, last)
                if boundary:
                    pe.wait_ge(w1_lo, KT)
                if not last:
                    subject_layer(n + 1)
                temporal_layer(n, first)
                if not last:
                    hidden(n + 1)
                else:
                    need(pe, soma_done, n * KT + KT)
                    need(pe, mod_th, n + 1)
                    for j in range(KT):
                        transpose_y(n, j, j)
                if first:
                    weights(END)
                output_layer(n, whole_k=1 if last else 2)
                if not last:
                    modulation(n + 1)
                    soma_layer(n + 1)

            subject_layer(0, first=True)
            weights(AT_N1 + 1)
            hidden(0)
            soma_layer(0, first=True)
            pe.wait_ge(n2_done, 1)
            pe.wait_ge(ident_done, 1)
            modulation(0)
            step(0, first=True)
            with pe.Fori(1, 3) as n:
                step(n)
            step(3, boundary=True)
            with pe.Fori(4, TILES - 1) as n:
                step(n)
            step(TILES - 1, last=True)

        @block.scalar
        def _(act):
            act.dma_start(vec[:], vecs).then_inc(small_in, 16)
            act.dma_start(sca[:], scal.partition_broadcast(P)).then_inc(small_in, 16)
            act.dma_start(w2raw[:], w_n2).then_inc(small_in, 16)
            act.dma_start(bn2[:], bn_2).then_inc(small_in, 16)

            def split_weight(i):
                if i < KT:
                    act.wait_ge(diag_done, i + 1)
                else:
                    act.wait_ge(stage_in[i % SLOTS], 16 * (i // SLOTS + 1))
                _, _, dst, scale = slices[i]
                act.activation(dst[:, HI], stage[i % SLOTS], ACT.Copy, scale=scale).then_inc(w_hi, 1)

            def split_x(n):
                need(act, x_in, n * 16)
                need(act, o_mm, (n - 1) * KT)
                for c in range(KT):
                    act.activation(xs_sgs[:, c, HI], xraw[:, c], ACT.Copy).then_inc(xh, 1)

            def make_y(n, b):
                need(act, gated, n * KT)
                need(act, yT_mm, n * KT)
                for o in range(KT):
                    need(act, l0_mm, n * KT + o + 1)
                    act.activation(y[:, o], psB[:, o], ACT.Identity, bias=bsubj[:, b, o:o + 1])
                    act.activation(ys[:, o, HI], psB[:, o], ACT.Identity, bias=bsubj[:, b, o:o + 1]).then_inc(y_hi, 1)

            def split_ctx(n, some):
                for i in some:
                    need(act, ctx_raw, n * KT + i + 1)
                    if i == 0:
                        need(act, g_mm, n * KT)
                    if i == 2:
                        need(act, t_mm, n * KT)
                    c = CTX_ORDER[i]
                    act.activation(cts[:, c, HI], tr0[:, c % 2], ACT.Copy).then_inc(ctx_hi, 1)

            def hidden(n):
                need(act, n1_mm, n + 1)
                need(act, h1_lo, n)
                need(act, mod_mm, n)
                act.activation(h1[:], psB[:, 0], ACT.Gelu, bias=vec[:, V_BN1:V_BN1 + 1])
                act.activation(h1s[:, HI], psB[:, 0], ACT.Gelu, bias=vec[:, V_BN1:V_BN1 + 1]).then_inc(h1_hi, 1)

            def modulation(n):
                need(act, mod_done, n * 16)
                need(act, mod_mm, n + 1)
                act.activation(mod_row[:], psB[0:D, 2], ACT.Tanh, bias=half_bn2[:], scale=0.5).then_inc(mod_th, 1)

            def soma_act(n, some=range(KT)):
                need(act, sg_raw, n * KT)
                for o in some:
                    need(act, s_mm, n * KT + o + 1)
                    act.activation(soma[:, o], psB[:, 1 - o % 2], ACT.Gelu, bias=vec[:, V_BSOMA + o:V_BSOMA + o + 1])\
                       .then_inc(soma_done, 1)

            def split_blend(n, c):
                need(act, blended, n * KT + c + 1)
                if c == 0:
                    need(act, t_mm, n * KT)
                if c == 2:
                    need(act, g_mm, n * KT + KT)
                act.activation(cts[:, tr_slot(c), HI], tr0[:, c % 2], ACT.Copy).then_inc(bl_hi, 1)

            def copy_residual(n, j, bank):
                need(act, yT_mm, n * KT + j + 1)
                act.activation(res[:, j], psB[:, bank], ACT.Copy).then_inc(res_copied, 1)

            def gates(n, late_x=None, last=False):
                need(act, sg_lo, n * KT)
                need(act, stored, n * KT * 16)
                for o in range(KT):
                    need(act, g_mm, n * KT + o + 1)
                    if o >= 2:
                        need(act, blended, n * KT + o - 1)
                    act.activation(th[:, o % 2], psA[:, o], ACT.Tanh, bias=half_b[:, V_BG + o:V_BG + o + 1], scale=0.5)\
                       .then_inc(g_th, 1)
                    if not last:
                        copy_residual(n, o, 2 + o % 2)
                    if o >= 1:
                        split_blend(n, o - 1)
                    if o == 1 and late_x is not None:
                        split_x(late_x)
                split_blend(n, KT - 1)

            def temporal_gates(n, last=False):
                for i in range(KT + 1):
                    if i < KT:
                        need(act, t_mm, n * KT + i + 1)
                        if i < 2:
                            need(act, blended, n * KT + i + 3)
                        else:
                            need(act, result, n * KT)
                        act.activation(gate_slots[i], psA[:, i], ACT.Tanh,
                                       bias=half_b[:, V_BTEMP + i:V_BTEMP + i + 1], scale=0.5).then_inc(t_th, 1)
                    if i >= 1:
                        need(act, sg_raw, n * KT + i)
                        act.activation(xs_sgs[:, i - 1, HI], gate_slots[i - 1], ACT.Copy).then_inc(sg_hi, 1)

            def step(n, b_next, last=False, boundary=False):
                if boundary:
                    for k in range(KT):
                        act.wait_ge(diag_done, KT + k + 1)
                        if k == 0:
                            need(act, l0_mm, n * KT + KT)
                        act.activation(wl0[:, k, HI], xraw[:, k], ACT.Copy).then_inc(w1_hi, 1)
                    gates(n, late_x=n + 1)
                else:
                    if not last:
                        split_x(n + 1)
                    gates(n, last=last)
                if not last:
                    make_y(n + 1, b_next)
                    split_ctx(n + 1, (0, 1))
                temporal_gates(n)
                if last:
                    for j in range(KT):
                        copy_residual(n, j, j)
                if not last:
                    hidden(n + 1)
                    split_ctx(n + 1, (2, 3))
                    modulation(n + 1)
                    soma_act(n + 1)

            for k in range(KT):
                act.wait_ge(x0_in[k], 16)
                act.activation(xs_sgs[:, k, HI], xraw[:, k], ACT.Copy).then_inc(xh, 1)
                split_weight(k)
            act.wait_ge(exp_ready, 1)
            act.activation(exps[:], sca[:], ACT.Exp).then_inc(exp_done, 1)
            act.activation(bexp[:], bexp[:], ACT.Exp).then_inc(exp_done, 1)
            act.activation(unused[:], sca[:, 0:1], ACT.Gelu)
            for i in range(AT_N1, AT_SOMA + 3):
                split_weight(i)
            act.wait_ge(bsubj_in, 16 * BATCH)
            make_y(0, 0)
            split_weight(AT_SOMA + 3)
            split_weight(AT_G)
            hidden(0)
            for i in (1, 2):
                split_weight(AT_G + i)
            soma_act(0, (0,))
            for i in (3, 4):
                split_weight(AT_G + i)
            soma_act(0, (1,))
            split_ctx(0, (0, 1))
            split_weight(AT_G + 5)
            soma_act(0, (2,))
            split_weight(AT_G + 6)
            soma_act(0, (3,))
            split_weight(AT_G + 7)
            act.wait_ge(setup, 1)
            modulation(0)
            split_ctx(0, (2, 3))
            for i in range(AT_TEMP, END):
                split_weight(i)
            act.wait_ge(w_lo, END)
            step(0, 0)
            with act.Fori(1, 3) as n:
                step(n, 0)
            step(3, 1, boundary=True)
            with act.Fori(4, TILES - 1) as n:
                step(n, 1)
            step(TILES - 1, 1, last=True)

        @block.gpsimd
        def _(pool):
            def add_beta(n):
                need(pool, bl_lo, n * KT + KT)
                for j in range(KT):
                    need(pool, res_copied, n * KT + j + 1)
                    pool.tensor_tensor(res[:, j], res[:, j], beta_b[:], ALU.add).then_inc(res_beta, 1)

            def inv_std(n):
                need(pool, result, n * KT)
                for j in range(KT):
                    need(pool, ln_mv, n * KT + j + 1)
                    pool.tensor_tensor(veps[:, j:j + 1], mv[:, j, 1:2], eps[:], ALU.add).then_inc(ln_eps, 1)
                    need(pool, ln_eps, n * KT + j + 1)
                    pool.tensor_tensor(rstd[:, j:j + 1], veps[:, j:j + 1], minus_half[:], ALU.pow).then_inc(ln_rstd, 1)

            pool.memset(ident[:], 0.0).then_inc(ident_zero, 1)
            pool.wait_ge(ident_zero, 1)
            pool.affine_select(out=ident[:], in_=ident[:], compare_op=ALU.not_equal, fill=1.0, base=0,
                               pattern=[[-1, P]], channel_multiplier=1).then_inc(ident_done, 1)
            pool.memset(eps[:], EPS)
            pool.memset(minus_half[:], -0.5).then_inc(mh_done, 1)
            pool.wait_ge(mh_done, 1)
            pool.wait_ge(affine_in, 32)

            def step(n):
                add_beta(n)
                inv_std(n)

            step(0)
            with pool.Fori(1, TILES) as n:
                step(n)

        @block.vector
        def _(dve):
            def stt(dst, a, s, b, op0, op1):
                return dve.scalar_tensor_tensor(out=dst, in0=a, scalar=s, in1=b, op0=op0, op1=op1)

            def minus(dst, a, hi):
                return dve.tensor_tensor(dst, a, bits(hi), ALU.subtract)

            links = [0]
            const = sem("const")

            def link(ins):
                links[0] += 1
                ins.then_inc(const, 1)
                dve.wait_ge(const, links[0])

            def small_constants():
                dve.memset(ctx_last[:], 0.0)
                dve.memset(w2wide[:], 0.0)
                link(dve.memset(tr_last[:], 0.0))
                dve.wait_ge(small_in, 16 * 4)
                bl = [vec[:, V_BLEND + d * KT:V_BLEND + (d + 1) * KT] for d in range(D)]
                link(dve.tensor_tensor(bmax[:], bl[0], bl[1], ALU.max))
                for d in range(D):
                    m = dve.tensor_tensor(bexp[:, d], bl[d], bmax[:], ALU.subtract)
                m.then_inc(exp_ready, 1)
                dve.tensor_scalar(half_bn2[:], bn2[:], 0.5, None, ALU.mult)
                dve.tensor_scalar(half_b[:], vec[:, 0:V_BN1], 0.5, None, ALU.mult).then_inc(setup, 1)
                link(dve.tensor_copy(w2wide[:, 0:D], w2raw[:]))
                dve.tensor_copy(wn2[:, HI], w2wide[:]).then_inc(n2_hi, 1)
                dve.wait_ge(n2_hi, 1)
                minus(wn2[:, LO], w2wide[:], wn2[:, HI]).then_inc(n2_done, 1)
                dve.wait_ge(exp_done, 2)
                link(dve.tensor_scalar(exps[:], exps[:], 1.0, None, ALU.add))
                link(dve.reciprocal(decay[:], exps[:]))
                link(dve.tensor_tensor(bsum[:], bexp[:, 0], bexp[:, 1], ALU.add))
                link(dve.reciprocal(bsum[:], bsum[:]))
                for d in range(D):
                    link(stt(blend[:, d], bexp[:, d], 0.25, bsum[:], ALU.mult, ALU.mult))

            def add_identity(buf, k):
                block_k = buf[:, k * P:(k + 1) * P]
                dve.tensor_tensor(block_k, block_k, ident[:], ALU.add).then_inc(diag_done, 1)

            def split_weight(i):
                _, _, dst, scale = slices[i]
                dve.wait_ge(w_hi, i + 1)
                if scale == 1.0:
                    minus(dst[:, LO], stage[i % SLOTS], dst[:, HI]).then_inc(w_lo, 1)
                else:
                    stt(dst[:, LO], stage[i % SLOTS], scale, bits(dst[:, HI]), ALU.mult, ALU.subtract).then_inc(w_lo, 1)

            def x_low(n, some=range(KT)):
                for c in some:
                    need(dve, xh, n * KT + c + 1)
                    minus(xs_sgs[:, c, LO], xraw[:, c], xs_sgs[:, c, HI]).then_inc(xl, 1)

            def y_low(n):
                for o in range(KT):
                    need(dve, y_hi, n * KT + o + 1)
                    minus(ys[:, o, LO], y[:, o], ys[:, o, HI]).then_inc(y_lo, 1)

            def context(n, some):
                if 0 in some:
                    need(dve, ctx_kept, n * KT)
                    need(dve, bl_lo, n * KT)
                else:
                    need(dve, ctx_lo, n * KT + 2)
                for i in some:
                    c = CTX_ORDER[i]
                    dve.tensor_tensor_scan(tr0[:, c % 2], decay[:, 0:1].to_broadcast([P, N]), y[:, c],
                                           ctx_last[:, c:c + 1], ALU.mult, ALU.add).then_inc(ctx_raw, 1)
                for i in some:
                    c = CTX_ORDER[i]
                    need(dve, ctx_raw, n * KT + i + 1)
                    dve.tensor_copy(ctx_last[:, c:c + 1], tr0[:, c % 2, N - 1:N]).then_inc(ctx_kept, 1)
                    need(dve, ctx_hi, n * KT + i + 1)
                    minus(cts[:, c, LO], tr0[:, c % 2], cts[:, c, HI]).then_inc(ctx_lo, 1)

            def hidden(n):
                need(dve, h1_hi, n + 1)
                minus(h1s[:, LO], h1[:], h1s[:, HI]).then_inc(h1_lo, 1)

            def modulation(n):
                need(dve, mod_th, n + 1)
                dve.tensor_scalar(mod_row[:], mod_row[:], 2.0, None, ALU.add).then_inc(mod_two, 1)

            def blend_low(n, c):
                need(dve, bl_hi, n * KT + c + 1)
                minus(cts[:, tr_slot(c), LO], tr0[:, c % 2], cts[:, tr_slot(c), HI]).then_inc(bl_lo, 1)

            def traces(n, boundary=False):
                STEPS = 6
                need(dve, mod_done, (n + 1) * 16)
                need(dve, trace, n * KT * STEPS)
                need(dve, blended, n * KT)
                need(dve, ctx_lo, n * KT + KT)
                for c in range(KT):
                    s = c % 2
                    base = n * KT * STEPS + c * STEPS
                    need(dve, g_th, n * KT + c + 1)
                    if c >= 1:
                        need(dve, blended, n * KT + c)
                    stt(th[:, s], th[:, s], 1.0, y[:, c], ALU.add, ALU.mult).then_inc(gated, 1)
                    need(dve, gated, n * KT + c + 1)
                    if c >= 2:
                        need(dve, bl_lo, n * KT + c - 1)
                    stt(tr0[:, s], th[:, s], blend[:, 0, c:c + 1], mod[:, 0], ALU.mult, ALU.mult).then_inc(trace, 1)
                    stt(tr1[:], th[:, s], blend[:, 1, c:c + 1], mod[:, 1], ALU.mult, ALU.mult).then_inc(trace, 1)
                    if c >= 1:
                        blend_low(n, c - 1)
                    for d, buf in enumerate((tr0[:, s], tr1[:])):
                        dve.wait_ge(trace, base + d + 1)
                        dve.tensor_tensor_scan(buf, decay[:, 1 + d:2 + d].to_broadcast([P, N]), buf,
                                               tr_last[:, d, c:c + 1], ALU.mult, ALU.add).then_inc(trace, 1)
                    for d, buf in enumerate((tr0[:, s], tr1[:])):
                        dve.wait_ge(trace, base + D + d + 1)
                        dve.tensor_copy(tr_last[:, d, c:c + 1], buf[:, N - 1:N]).then_inc(trace, 1)
                    dve.wait_ge(trace, base + D + D + 1)
                    dve.tensor_tensor(tr0[:, s], tr0[:, s], tr1[:], ALU.add).then_inc(blended, 1)
                    if boundary and c == 1:
                        x_low(n + 1)
                blend_low(n, KT - 1)

            def soma_gate(n):
                need(dve, soma_done, n * KT + KT)
                for c in range(KT + 1):
                    if c < KT:
                        need(dve, t_th, n * KT + c + 1)
                        stt(gate_slots[c], gate_slots[c], 1.0, soma[:, c], ALU.add, ALU.mult).then_inc(sg_raw, 1)
                    if c >= 1:
                        need(dve, sg_hi, n * KT + c)
                        minus(xs_sgs[:, c - 1, LO], gate_slots[c - 1], xs_sgs[:, c - 1, HI]).then_inc(sg_lo, 1)

            def norm(n):
                def stats_of(j):
                    need(dve, o_mm, n * KT + j + 1)
                    dve.bn_stats(stats[:, j], psA[:, j]).then_inc(ln_stats, 1)

                def aggregate(j):
                    dve.bn_aggr(mv[:, j], stats[:, j]).then_inc(ln_mv, 1)

                def centre(j):
                    need(dve, ln_mv, n * KT + j + 1)
                    stt(normed[:, j % 2], psA[:, j], mv[:, j, 0:1], gamma_b[:], ALU.subtract, ALU.mult)\
                        .then_inc(ln_centred, 1)

                def finish(j):
                    need(dve, ln_centred, n * KT + j + 1)
                    need(dve, res_beta, n * KT + j + 1)
                    need(dve, ln_rstd, n * KT + j + 1)
                    stt(res[:, j], normed[:, j % 2], rstd[:, j:j + 1], res[:, j], ALU.mult, ALU.add)\
                        .then_inc(result, 1)

                need(dve, ln_rstd, n * KT)
                need(dve, sg_lo, n * KT + KT)
                stats_of(0)
                for j in range(1, KT):
                    need(dve, ln_stats, n * KT + j)
                    stats_of(j)
                    aggregate(j - 1)
                    if j >= 3:
                        need(dve, result, n * KT + j - 2)
                    centre(j - 1)
                    if j == 2:
                        finish(0)
                need(dve, ln_stats, n * KT + KT)
                finish(1)
                aggregate(KT - 1)
                need(dve, result, n * KT + 2)
                centre(KT - 1)
                finish(2)
                finish(3)

            def second_weights_low():
                for k in range(KT):
                    dve.wait_ge(w1_hi, k + 1)
                    minus(wl0[:, k, LO], xraw[:, k], wl0[:, k, HI]).then_inc(w1_lo, 1)
                dve.wait_ge(ctx_kept, TPB * KT)
                link(dve.memset(ctx_last[:], 0.0))

            def step(n, last=False, boundary=False):
                if boundary:
                    second_weights_low()
                elif not last:
                    x_low(n + 1)
                traces(n, boundary)
                if not last:
                    y_low(n + 1)
                    context(n + 1, (0, 1))
                soma_gate(n)
                if not last:
                    hidden(n + 1)
                    context(n + 1, (2, 3))
                norm(n)
                if not last:
                    modulation(n + 1)

            dve.wait_ge(ident_done, 1)
            for k in range(KT):
                x_low(0, (k,))
                dve.wait_ge(stage_in[k], 16)
                add_identity(stage[k], k)
                split_weight(k)
            small_constants()
            for i in range(AT_N1, AT_SOMA + 3):
                split_weight(i)
            y_low(0)
            split_weight(AT_SOMA + 3)
            split_weight(AT_G)
            hidden(0)
            for i in range(1, 5):
                split_weight(AT_G + i)
            context(0, (0, 1))
            for i in range(5, 8):
                split_weight(AT_G + i)
            modulation(0)
            context(0, (2, 3))
            for i in range(AT_TEMP, END):
                split_weight(i)
            dve.wait_ge(w_lo, END)
            step(0)
            with dve.Fori(1, 3) as n:
                step(n)
            dve.wait_ge(w1_in, 16)
            for k in range(KT):
                add_identity(xraw[:, k], k)

            step(3, boundary=True)
            dve.wait_ge(trace, TPB * KT * 6)
            link(dve.memset(tr_last[:], 0.0))
            with dve.Fori(4, TILES - 1) as n:
                step(n)
            step(TILES - 1, last=True)


def kernel(x, itok_B_0_7, condB_tauraws, cond_256, condB_bn2, cond_1024, L0_cond_weight, L0_cond_bias,
           L1_cond_tau_ctx, L1_cond_Wg, L1_cond_bg, L1_cond_Wn1, L1_cond_bn1, L1_cond_Wsoma, L1_cond_bsoma,
           L1_cond_Wtemp, L1_cond_btemp, L1_cond_Wout, L1_cond_gamma, L1_cond_beta):
    import numpy as np
    import concourse.bacc as bacc
    from concourse.bass_utils import run_bass_kernel_spmd

    def rows(w):
        w = np.asarray(w)
        return np.ascontiguousarray(w.T.reshape(-1, P, w.shape[0]))

    def chan(v):
        return np.asarray(v).reshape(-1, P).T

    subj = np.asarray(L0_cond_weight)
    arrays = {
        "x_t": np.ascontiguousarray(np.asarray(x).reshape(TILES, N, KT, P).transpose(0, 3, 2, 1)),
        "ids": np.asarray(itok_B_0_7).reshape(1, BATCH),
        "w_subj": np.ascontiguousarray(subj.transpose(0, 2, 1).reshape(subj.shape[0], KT, P, E)),
        "b_subj": np.ascontiguousarray(np.asarray(L0_cond_bias).reshape(-1, KT, P).transpose(0, 2, 1)),
        "w_g": rows(L1_cond_Wg),
        "w_n1": np.ascontiguousarray(rows(L1_cond_Wn1).transpose(1, 0, 2).reshape(1, P, E)),
        "w_n2": np.ascontiguousarray(np.asarray(cond_256).T),
        "w_soma": rows(L1_cond_Wsoma),
        "w_temp": rows(L1_cond_Wtemp),
        "w_out": rows(L1_cond_Wout),
        "vecs": np.ascontiguousarray(np.concatenate(
            [chan(L1_cond_bg), chan(L1_cond_bsoma), chan(L1_cond_btemp), chan(L1_cond_bn1),
             *[chan(row) for row in np.asarray(cond_1024)]], axis=1)),
        "scal": np.concatenate([np.asarray(L1_cond_tau_ctx).reshape(1), np.asarray(condB_tauraws)]),
        "bn_2": np.asarray(condB_bn2).reshape(D, 1),
        "gamma": np.asarray(L1_cond_gamma),
        "beta": np.asarray(L1_cond_beta),
    }
    nc = bacc.Bacc("TRN2", target_bir_lowering=False, num_devices=1, dynamic_dma_scratch_size=1024)
    aps = {k: nc.dram_tensor(f"in_{k}", a.shape, mybir.dt.from_np(a.dtype), kind="ExternalInput").ap()
           for k, a in arrays.items()}
    out = nc.dram_tensor("out_0", (BATCH, SEQ, E), F32, kind="ExternalOutput").ap()
    build(nc, **aps, out=out)
    r = run_bass_kernel_spmd(nc, [{f"in_{k}": a for k, a in arrays.items()}], core_ids=[0])
    return r.results[0]["out_0"]
```

```python
from contextlib import ExitStack

import concourse.bass as bass
from concourse import mybir

P = 128
E = 512
KT = E // P
N = 512
D = 2
BATCH = 2
SEQ = 2048
TPB = SEQ // N
TILES = BATCH * TPB
HI, LO = 0, 1
EPS = 1e-5

ALU = mybir.AluOpType
ACT = mybir.ActivationFunctionType
F32 = mybir.dt.float32
F32R = mybir.dt.float32r

CTX_ORDER = (2, 3, 0, 1)

QUADS = 4
QP = P // QUADS
WARM_UPS = 14
PAIR = 2

V_BG, V_BSOMA, V_BTEMP, V_BN1, V_BLEND = 0, 4, 8, 12, 13
V_COLS = 21
S_COLS = 1 + D


def build(nc, x_t, ids, w_subj, b_subj, w_g, w_n1, w_n2, w_soma, w_temp, w_out, vecs, scal, bn_2, gamma, beta, out):
    mod_dram = nc.dram_tensor("mod_rows", (D * N,), F32).ap()
    out_v = out.rearrange("b (t j p) e -> (b t) j p e", p=P, j=KT)

    with ExitStack() as ctx:
        def sb(name, shape, dt=F32):
            return ctx.enter_context(nc.sbuf_tensor(name, shape, dt))

        def sem(name):
            return ctx.enter_context(nc.semaphore(name))

        wl0 = sb("wl0", [P, KT, 2, E], F32R)
        wg = sb("wg", [P, 2 * KT, 2, E], F32R)
        wn1 = sb("wn1", [P, 1, 2, E], F32R)
        wn2 = sb("wn2", [P, 2, P], F32R)
        wsoma = sb("wsoma", [P, KT, 2, E], F32R)
        wtemp = sb("wtemp", [P, KT, 2, E], F32R)
        wout = sb("wout", [P, KT, 2, E], F32R)
        xs_sgs = sb("xs_sgs", [P, KT, 2, N], F32R)
        ys = sb("ys", [P, KT, 2, N], F32R)
        cts = sb("cts", [P, KT + 2, 2, N], F32R)
        h1s = sb("h1s", [P, 2, N], F32R)
        xraw = sb("xraw", [P, KT, N])
        y = sb("y", [P, KT, N])
        soma = sb("soma", [P, KT, N])
        res = sb("res", [P, KT, E])
        th = sb("th", [P, 2, N])
        tr0 = sb("tr0", [P, 2, N])
        tr1 = sb("tr1", [P, N])
        h1 = sb("h1", [P, N])
        mod_row = sb("mod_row", [D, N])
        mod = sb("mod", [P, D, N])
        normed = sb("normed", [P, 2, E])
        ident = sb("ident", [P, P])
        gamma_b = sb("gamma_b", [P, E])
        beta_b = sb("beta_b", [P, E])
        vec = sb("vec", [P, V_COLS])
        half_b = sb("half_b", [P, V_BN1])
        bsubj = sb("bsubj", [P, BATCH, KT])
        w2raw = sb("w2raw", [P, D])
        w2wide = sb("w2wide", [P, P])
        unused = sb("unused", [P, 1])
        sca = sb("sca", [P, S_COLS])
        bn2 = sb("bn2", [D, 1])
        half_bn2 = sb("half_bn2", [D, 1])
        decay = sb("decay", [P, 1 + D])
        exps = sb("exps", [P, 1 + D])
        bmax = sb("bmax", [P, KT])
        bexp = sb("bexp", [P, D, KT])
        bsum = sb("bsum", [P, KT])
        blend = sb("blend", [P, D, KT])
        minus_half = sb("minus_half", [P, 1])
        eps = sb("eps", [P, 1])
        ctx_last = sb("ctx_last", [P, KT])
        tr_last = sb("tr_last", [P, D, KT])
        stats = sb("stats", [P, KT, 6])
        mv = sb("mv", [P, KT, 2])
        veps = sb("veps", [P, KT])
        rstd = sb("rstd", [P, KT])
        idt = sb("idt", [1, BATCH], mybir.dt.int32)

        psA = ctx.enter_context(nc.psum_tensor("psA", [P, KT, N], F32))
        psB = ctx.enter_context(nc.psum_tensor("psB", [P, KT, N], F32))

        ids_in, small_in, bsubj_in, affine_in = (sem(f"{n}_in") for n in ("ids", "small", "bsubj", "affine"))
        x0_in = [sem(f"x0_in{c}") for c in range(KT)]
        x_in = sem("x_in")
        w1_in = sem("w1_in")
        stored = sem("stored")
        SLOTS = 8
        stage_in = [sem(f"stage_in{s}") for s in range(SLOTS)]
        ident_zero, ident_done = sem("ident_zero"), sem("ident_done")
        diag_done = sem("diag_done")
        w_hi, w_lo = sem("w_hi"), sem("w_lo")
        w1_hi, w1_lo = sem("w1_hi"), sem("w1_lo")
        n2_hi, n2_done = sem("n2_hi"), sem("n2_done")
        setup = sem("setup")
        mh_done = sem("mh_done")
        exp_ready, exp_done = sem("exp_ready"), sem("exp_done")
        xh, xl = sem("xh"), sem("xl")
        l0_mm, g_mm, t_mm, s_mm, o_mm = (sem(f"{n}_mm") for n in ("l0", "g", "t", "s", "o"))
        n1_mm, mod_mm = sem("n1_mm"), sem("mod_mm")
        y_hi, y_lo = sem("y_hi"), sem("y_lo")
        y0_sum = sem("y0_sum")
        ctx_raw, ctx_hi, ctx_lo, ctx_kept = (sem(f"ctx_{n}") for n in ("raw", "hi", "lo", "kept"))
        h1_hi, h1_lo = sem("h1_hi"), sem("h1_lo")
        mod_th, mod_two = sem("mod_th"), sem("mod_two")
        mod_sent, mod_done = sem("mod_sent"), sem("mod_done")
        soma_done = sem("soma_done")
        g_th, gated = sem("g_th"), sem("gated")
        trace = sem("trace")
        blended, bl_hi, bl_lo = sem("blended"), sem("bl_hi"), sem("bl_lo")
        t_th, sg_raw, sg_hi, sg_lo = sem("t_th"), sem("sg_raw"), sem("sg_hi"), sem("sg_lo")
        turned, res_in, res_beta = sem("turned"), sem("res_in"), sem("res_beta")
        ln_stats, ln_mv, ln_centred, ln_eps, ln_rstd, result = (
            sem(f"ln_{n}") for n in ("stats", "mv", "centred", "eps", "rstd", "result"))

        def need(eng, semaphore, count):
            if not (isinstance(count, int) and count <= 0):
                eng.wait_ge(semaphore, count)

        def bits(ap):
            return ap.bitcast(F32)

        slices = ([("subj", k, wl0[:, k], 1.0) for k in range(KT)]
                  + [(w_n1, 0, wn1[:, 0], 1.0)]
                  + [(w_soma, k, wsoma[:, k], 1.0) for k in range(KT)]
                  + [(w_g, k, wg[:, k], 1.0) for k in range(2 * KT)]
                  + [(w_temp, k, wtemp[:, k], 1.0) for k in range(KT)]
                  + [(w_out, k, wout[:, k], 0.5) for k in range(KT)])
        AT_L0, AT_N1, AT_SOMA, AT_G, AT_TEMP, AT_OUT = 0, 4, 5, 9, 17, 21
        END = len(slices)
        stage = [res[:, 0], res[:, 1], res[:, 2], res[:, 3], th[:, 0], th[:, 1], normed[:, 0], normed[:, 1]]

        block = ctx.enter_context(nc.Block())

        gate_slots = [th[:, 0], th[:, 1], normed[:, 0], normed[:, 1]]

        turning = normed[:].rearrange("p i e -> p (i e)").rearrange("p (b i c) -> p b i c", b=P // QP, i=PAIR)
        RES_DMAS = KT // PAIR * QUADS

        def tr_slot(c):
            return KT + c if c < 2 else c - 2

        @block.sync
        def _(sp):
            sp.dma_start(idt[:], ids).then_inc(ids_in, 16)

            def load_x0(c):
                sp.dma_start(xraw[:, c], x_t[0, :, c]).then_inc(x0_in[c], 16)

            load_x0(0)
            sp.wait_ge(ids_in, 16)
            sid = [sp.value_load(idt[0:1, b:b + 1], min_val=0, max_val=w_subj.shape[0] - 1) for b in range(BATCH)]
            for i, (src, k, _, _) in enumerate(slices):
                if i >= SLOTS:
                    sp.wait_ge(w_lo, i - SLOTS + 1)
                rows_k = w_subj[bass.ds(sid[0], 1), k].rearrange("s p e -> p (s e)") if src == "subj" else src[k]
                sp.dma_start(stage[i % SLOTS], rows_k).then_inc(stage_in[i % SLOTS], 16)
                if i + 1 < KT:
                    load_x0(i + 1)
                if i == AT_N1:
                    for b in range(BATCH):
                        sp.dma_start(bsubj[:, b], b_subj[bass.ds(sid[b], 1)].rearrange("s p k -> p (s k)"))\
                          .then_inc(bsubj_in, 16)
            sp.dma_start(gamma_b[:], gamma.partition_broadcast(P)).then_inc(affine_in, 16)
            sp.dma_start(beta_b[:], beta.partition_broadcast(P)).then_inc(affine_in, 16)

            def load_x(n):
                sp.wait_ge(xl, n * KT)
                sp.dma_start(xraw[:], x_t[bass.ds(n, 1)].rearrange("a p k t -> p (a k) t")).then_inc(x_in, 16)

            def store(n):
                for j in range(KT):
                    sp.wait_ge(result, n * KT + j + 1)
                    sp.dma_start(out_v[bass.ds(n, 1), j].rearrange("a p e -> p (a e)"), res[:, j]).then_inc(stored, 16)

            def spread_mod(n):
                need(sp, mod_two, n + 1)
                sp.dma_start(mod_dram.rearrange("(d n) -> d n", d=D), mod_row[:]).then_inc(mod_sent, 16)
                need(sp, mod_sent, (n + 1) * 16)
                need(sp, blended, n * KT)
                sp.dma_start(mod[:].rearrange("p d n -> p (d n)"), mod_dram.partition_broadcast(P)).then_inc(mod_done, 16)

            def residual(n):
                for i in range(KT // PAIR):
                    need(sp, turned, n * KT + (i + 1) * PAIR)
                    for q in range(QUADS):
                        sp.dma_start(res[:, i * PAIR:(i + 1) * PAIR, q * P:(q + 1) * P],
                                     turning[q * QP:(q + 1) * QP]).then_inc(res_in, 16)

            load_x(1)
            spread_mod(0)
            residual(0)
            with sp.Fori(0, 2) as n:
                load_x(n + 2)
                store(n)
                spread_mod(n + 1)
                residual(n + 1)
            sp.wait_ge(xl, 4 * KT)
            sp.dma_start(xraw[:], w_subj[bass.ds(sid[1], 1)].rearrange("s k p e -> p (s k) e")).then_inc(w1_in, 16)
            store(2)
            spread_mod(3)
            sp.wait_ge(w1_lo, KT)
            load_x(4)
            residual(3)
            load_x(5)
            store(3)
            spread_mod(4)
            residual(4)
            with sp.Fori(4, 6) as n:
                load_x(n + 2)
                store(n)
                spread_mod(n + 1)
                residual(n + 1)
            store(6)
            spread_mod(7)
            residual(7)
            store(7)
            sp.wait_ge(stored, TILES * KT * 16)

        @block.tensor
        def _(pe):
            def split_mm(dst, w, a, start, stop):
                pe.matmul(dst, w[HI], a[HI], start=start, stop=False)
                pe.matmul(dst, w[HI], a[LO], start=False, stop=False)
                return pe.matmul(dst, w[LO], a[HI], start=False, stop=stop)

            def cols(w, k, o):
                return [w[:, k, h, o * P:(o + 1) * P] for h in (HI, LO)]

            def pair(a, k):
                return [a[:, k, h] for h in (HI, LO)]

            def weights(count):
                pe.wait_ge(w_lo, count)

            def first_subject_layer():
                for k in range(KT - 1):
                    pe.wait_ge(w_hi, AT_L0 + k + 1)
                    pe.wait_ge(xl, k + 1)
                    for o in range(KT):
                        pe.matmul(psB[:, o], cols(wl0, k, o)[HI], xs_sgs[:, k, HI], start=k == 0, stop=False)
                        pe.matmul(psB[:, o], cols(wl0, k, o)[HI], xs_sgs[:, k, LO], start=False, stop=False)
                    weights(AT_L0 + k + 1)
                    for o in range(KT):
                        pe.matmul(psB[:, o], cols(wl0, k, o)[LO], xs_sgs[:, k, HI], start=False, stop=False)
                weights(AT_L0 + KT)
                pe.wait_ge(xl, KT)
                for o in range(KT):
                    split_mm(psB[:, o], cols(wl0, KT - 1, o), pair(xs_sgs, KT - 1), False, True).then_inc(l0_mm, 1)

            def subject_layer(n):
                need(pe, soma_done, n * KT)
                for k in range(KT):
                    need(pe, xl, n * KT + k + 1)
                    for o in range(KT):
                        if k == 0 and o == 2:
                            need(pe, mod_th, n)
                        m = split_mm(psB[:, o], cols(wl0, k, o), pair(xs_sgs, k), k == 0, k == KT - 1)
                        if k == KT - 1:
                            m.then_inc(l0_mm, 1)

            def hidden(n):
                for k in range(KT):
                    need(pe, y_lo, n * KT + k + 1)
                    m = split_mm(psB[:, 0], [wn1[:, 0, h, k * P:(k + 1) * P] for h in (HI, LO)], pair(ys, k),
                                 k == 0, k == KT - 1)
                m.then_inc(n1_mm, 1)

            def modulation(n):
                need(pe, h1_lo, n + 1)
                split_mm(psB[:, 2], [wn2[:, h] for h in (HI, LO)], [h1s[:, h] for h in (HI, LO)],
                         True, True).then_inc(mod_mm, 1)

            def soma_layer(n, first=False):
                for o in range(KT):
                    if o == 1:
                        need(pe, h1_hi, n + 1)
                    if o >= 2:
                        need(pe, soma_done, n * KT + o - 1)
                    for k in range(KT):
                        if first and o == 0:
                            weights(AT_SOMA + k + 1)
                        m = split_mm(psB[:, 1 - o % 2], cols(wsoma, k, o), pair(ys, k), k == 0, k == KT - 1)
                    m.then_inc(s_mm, 1)

            def gate_layer(n, first=False):
                for o in range(KT):
                    if o == 0:
                        need(pe, ln_centred, n * KT)
                    for k in range(KT):
                        if first and o == 0:
                            weights(AT_G + k + 1)
                        split_mm(psA[:, o], cols(wg, k, o), pair(ys, k), k == 0, False)
                    for i, k in enumerate(CTX_ORDER):
                        if o == 0:
                            need(pe, ctx_lo, n * KT + i + 1)
                            if first:
                                weights(AT_G + 2 * KT)
                        m = split_mm(psA[:, o], cols(wg, KT + k, o), pair(cts, k), False, i == KT - 1)
                    m.then_inc(g_mm, 1)

            def temporal_layer(n, first=False):
                for k in range(KT):
                    if first:
                        weights(AT_TEMP + k + 1)
                    need(pe, bl_lo, n * KT + k + 1)
                    for o in range(KT):
                        if k == 0:
                            need(pe, g_th, n * KT + o + 1)
                        m = split_mm(psA[:, o], cols(wtemp, k, o), pair(cts, tr_slot(k)), k == 0, k == KT - 1)
                        if k == KT - 1:
                            m.then_inc(t_mm, 1)

            def output_layer(n, early):
                def with_high(k, j):
                    a = xs_sgs[:, k, HI, j * P:(j + 1) * P]
                    pe.matmul(psA[:, j], a, wout[:, k, HI], start=k == 0, stop=False)
                    pe.matmul(psA[:, j], a, wout[:, k, LO], start=False, stop=False)

                def with_low(k, j):
                    return pe.matmul(psA[:, j], xs_sgs[:, k, LO, j * P:(j + 1) * P], wout[:, k, HI],
                                     start=False, stop=k == KT - 1)

                for k, row_tiles in enumerate(early):
                    need(pe, sg_hi, n * KT + k + 1)
                    for j in row_tiles:
                        if k == 0:
                            need(pe, t_th, n * KT + j + 1)
                        with_high(k, j)
                    need(pe, sg_lo, n * KT + k + 1)
                    for j in row_tiles:
                        with_low(k, j)
                need(pe, sg_lo, n * KT + KT)
                for j in range(KT):
                    for k in range(KT):
                        if k >= len(early) or j not in early[k]:
                            with_high(k, j)
                            m = with_low(k, j)
                    m.then_inc(o_mm, 1)

            def step(n, first=False, last=False, boundary=False):
                gate_layer(n, first)
                if boundary:
                    pe.wait_ge(w1_lo, KT)
                if not last:
                    subject_layer(n + 1)
                temporal_layer(n, first)
                if not last:
                    hidden(n + 1)
                if first:
                    weights(END)
                output_layer(n, early=(range(KT), range(2) if last else range(KT)))
                if not last:
                    modulation(n + 1)
                    soma_layer(n + 1)

            pe.wait_ge(ident_done, 1)
            for _ in range(WARM_UPS):
                pe.matmul(psA[:, 0, 0:P], ident[:], ident[:], start=True, stop=True)
            first_subject_layer()
            weights(AT_N1 + 1)
            hidden(0)
            soma_layer(0, first=True)
            pe.wait_ge(n2_done, 1)
            modulation(0)
            step(0, first=True)
            with pe.Fori(1, 3) as n:
                step(n)
            step(3, boundary=True)
            with pe.Fori(4, TILES - 1) as n:
                step(n)
            step(TILES - 1, last=True)

        @block.scalar
        def _(act):
            act.dma_start(vec[:], vecs).then_inc(small_in, 16)
            act.dma_start(sca[:], scal.partition_broadcast(P)).then_inc(small_in, 16)
            act.dma_start(w2raw[:], w_n2).then_inc(small_in, 16)
            act.dma_start(bn2[:], bn_2).then_inc(small_in, 16)

            def split_weight(i):
                if i < KT:
                    act.wait_ge(diag_done, i + 1)
                else:
                    act.wait_ge(stage_in[i % SLOTS], 16 * (i // SLOTS + 1))
                _, _, dst, scale = slices[i]
                act.activation(dst[:, HI], stage[i % SLOTS], ACT.Copy, scale=scale).then_inc(w_hi, 1)

            def split_x(n):
                need(act, x_in, n * 16)
                need(act, o_mm, (n - 1) * KT)
                for c in range(KT):
                    act.activation(xs_sgs[:, c, HI], xraw[:, c], ACT.Copy).then_inc(xh, 1)

            def high_y0():
                for o in range(KT):
                    act.wait_ge(l0_mm, o + 1)
                    act.activation(ys[:, o, HI], psB[:, o], ACT.Identity, bias=bsubj[:, 0, o:o + 1]).then_inc(y_hi, 1)

            def make_y(n, b):
                need(act, gated, n * KT)
                need(act, turned, n * KT)
                for o in range(KT):
                    need(act, l0_mm, n * KT + o + 1)
                    act.activation(y[:, o], psB[:, o], ACT.Identity, bias=bsubj[:, b, o:o + 1])
                    act.activation(ys[:, o, HI], psB[:, o], ACT.Identity, bias=bsubj[:, b, o:o + 1]).then_inc(y_hi, 1)

            def split_ctx(n, some):
                for i in some:
                    need(act, ctx_raw, n * KT + i + 1)
                    if i == 0:
                        need(act, g_mm, n * KT)
                    if i == 2:
                        need(act, t_mm, n * KT)
                    c = CTX_ORDER[i]
                    act.activation(cts[:, c, HI], tr0[:, c % 2], ACT.Copy).then_inc(ctx_hi, 1)

            def hidden(n):
                need(act, n1_mm, n + 1)
                need(act, h1_lo, n)
                need(act, mod_mm, n)
                act.activation(h1[:], psB[:, 0], ACT.Gelu, bias=vec[:, V_BN1:V_BN1 + 1])
                act.activation(h1s[:, HI], psB[:, 0], ACT.Gelu, bias=vec[:, V_BN1:V_BN1 + 1]).then_inc(h1_hi, 1)

            def modulation(n):
                need(act, mod_done, n * 16)
                need(act, mod_mm, n + 1)
                act.activation(mod_row[:], psB[0:D, 2], ACT.Tanh, bias=half_bn2[:], scale=0.5).then_inc(mod_th, 1)

            def soma_act(n, some=range(KT)):
                need(act, sg_raw, n * KT)
                for o in some:
                    need(act, s_mm, n * KT + o + 1)
                    act.activation(soma[:, o], psB[:, 1 - o % 2], ACT.Gelu, bias=vec[:, V_BSOMA + o:V_BSOMA + o + 1])\
                       .then_inc(soma_done, 1)

            def split_blend(n, c):
                need(act, blended, n * KT + c + 1)
                if c == 0:
                    need(act, t_mm, n * KT)
                if c == 2:
                    need(act, g_mm, n * KT + KT)
                act.activation(cts[:, tr_slot(c), HI], tr0[:, c % 2], ACT.Copy).then_inc(bl_hi, 1)

            def gates(n, late_x=None):
                need(act, sg_lo, n * KT)
                for o in range(KT):
                    need(act, g_mm, n * KT + o + 1)
                    if o >= 2:
                        need(act, blended, n * KT + o - 1)
                    act.activation(th[:, o % 2], psA[:, o], ACT.Tanh, bias=half_b[:, V_BG + o:V_BG + o + 1], scale=0.5)\
                       .then_inc(g_th, 1)
                    if o >= 1:
                        split_blend(n, o - 1)
                    if o == 1 and late_x is not None:
                        split_x(late_x)
                split_blend(n, KT - 1)

            def temporal_gates(n):
                def gate(i):
                    need(act, t_mm, n * KT + i + 1)
                    if i < 2:
                        need(act, blended, n * KT + i + 3)
                    else:
                        need(act, res_in, (n + 1) * RES_DMAS * 16)
                    act.activation(gate_slots[i], psA[:, i], ACT.Tanh,
                                   bias=half_b[:, V_BTEMP + i:V_BTEMP + i + 1], scale=0.5).then_inc(t_th, 1)

                def high(i):
                    need(act, sg_raw, n * KT + i + 1)
                    act.activation(xs_sgs[:, i, HI], gate_slots[i], ACT.Copy).then_inc(sg_hi, 1)

                gate(0)
                gate(1)
                high(0)
                gate(2)
                gate(3)
                for i in range(1, KT):
                    high(i)

            def step(n, b_next, last=False, boundary=False):
                if boundary:
                    for k in range(KT):
                        act.wait_ge(diag_done, KT + k + 1)
                        if k == 0:
                            need(act, l0_mm, n * KT + KT)
                        act.activation(wl0[:, k, HI], xraw[:, k], ACT.Copy).then_inc(w1_hi, 1)
                    gates(n, late_x=n + 1)
                else:
                    if not last:
                        split_x(n + 1)
                    gates(n)
                if not last:
                    make_y(n + 1, b_next)
                    split_ctx(n + 1, (0, 1))
                temporal_gates(n)
                if not last:
                    hidden(n + 1)
                    split_ctx(n + 1, (2, 3))
                    modulation(n + 1)
                    soma_act(n + 1)

            def high_x0(k):
                act.wait_ge(x0_in[k], 16)
                act.activation(xs_sgs[:, k, HI], xraw[:, k], ACT.Copy).then_inc(xh, 1)

            high_x0(0)
            for k in range(KT):
                split_weight(k)
                if k + 1 < KT:
                    high_x0(k + 1)
                if k == KT - 2:
                    act.wait_ge(exp_ready, 1)
                    act.activation(exps[:], sca[:], ACT.Exp).then_inc(exp_done, 1)
                    act.activation(bexp[:], bexp[:], ACT.Exp).then_inc(exp_done, 1)
                    act.activation(unused[:], sca[:, 0:1], ACT.Gelu)
            for i in range(AT_N1, AT_SOMA + 3):
                split_weight(i)
            act.wait_ge(bsubj_in, 16 * BATCH)
            high_y0()
            split_weight(AT_SOMA + 3)
            split_weight(AT_G)
            hidden(0)
            for i in (1, 2):
                split_weight(AT_G + i)
            soma_act(0, (0,))
            for i in (3, 4):
                split_weight(AT_G + i)
            soma_act(0, (1,))
            split_ctx(0, (0, 1))
            split_weight(AT_G + 5)
            soma_act(0, (2,))
            split_weight(AT_G + 6)
            soma_act(0, (3,))
            split_weight(AT_G + 7)
            act.wait_ge(setup, 1)
            modulation(0)
            split_ctx(0, (2, 3))
            for i in range(AT_TEMP, END):
                split_weight(i)
            act.wait_ge(w_lo, END)
            step(0, 0)
            with act.Fori(1, 3) as n:
                step(n, 0)
            step(3, 1, boundary=True)
            with act.Fori(4, TILES - 1) as n:
                step(n, 1)
            step(TILES - 1, 1, last=True)

        @block.gpsimd
        def _(pool):
            def add_beta(n):
                need(pool, bl_lo, n * KT + KT)
                need(pool, res_in, (n + 1) * RES_DMAS * 16)
                for j in range(KT):
                    pool.tensor_tensor(res[:, j], res[:, j], beta_b[:], ALU.add).then_inc(res_beta, 1)

            def inv_std(n):
                need(pool, result, n * KT)
                for j in range(KT):
                    need(pool, ln_mv, n * KT + j + 1)
                    pool.tensor_tensor(veps[:, j:j + 1], mv[:, j, 1:2], eps[:], ALU.add).then_inc(ln_eps, 1)
                    need(pool, ln_eps, n * KT + j + 1)
                    pool.tensor_tensor(rstd[:, j:j + 1], veps[:, j:j + 1], minus_half[:], ALU.pow).then_inc(ln_rstd, 1)

            pool.memset(ident[:], 0.0).then_inc(ident_zero, 1)
            pool.wait_ge(ident_zero, 1)
            pool.affine_select(out=ident[:], in_=ident[:], compare_op=ALU.not_equal, fill=1.0, base=0,
                               pattern=[[-1, P]], channel_multiplier=1).then_inc(ident_done, 1)
            pool.memset(eps[:], EPS)
            pool.memset(minus_half[:], -0.5).then_inc(mh_done, 1)
            pool.wait_ge(mh_done, 1)
            for o in range(KT):
                pool.wait_ge(y_lo, o + 1)
                pool.tensor_tensor(y[:, o], bits(ys[:, o, HI]), bits(ys[:, o, LO]), ALU.add).then_inc(y0_sum, 1)
            pool.wait_ge(affine_in, 32)

            def step(n):
                add_beta(n)
                inv_std(n)

            step(0)
            with pool.Fori(1, TILES) as n:
                step(n)

        @block.vector
        def _(dve):
            def stt(dst, a, s, b, op0, op1):
                return dve.scalar_tensor_tensor(out=dst, in0=a, scalar=s, in1=b, op0=op0, op1=op1)

            def minus(dst, a, hi):
                return dve.tensor_tensor(dst, a, bits(hi), ALU.subtract)

            links = [0]
            const = sem("const")

            def link(ins):
                links[0] += 1
                ins.then_inc(const, 1)
                dve.wait_ge(const, links[0])

            def small_constants():
                dve.memset(ctx_last[:], 0.0)
                dve.memset(w2wide[:], 0.0)
                link(dve.memset(tr_last[:], 0.0))
                dve.wait_ge(small_in, 16 * 4)
                bl = [vec[:, V_BLEND + d * KT:V_BLEND + (d + 1) * KT] for d in range(D)]
                link(dve.tensor_tensor(bmax[:], bl[0], bl[1], ALU.max))
                for d in range(D):
                    m = dve.tensor_tensor(bexp[:, d], bl[d], bmax[:], ALU.subtract)
                m.then_inc(exp_ready, 1)
                dve.tensor_scalar(half_bn2[:], bn2[:], 0.5, None, ALU.mult)
                dve.tensor_scalar(half_b[:], vec[:, 0:V_BN1], 0.5, None, ALU.mult).then_inc(setup, 1)

            def decays_and_blend():
                link(dve.tensor_copy(w2wide[:, 0:D], w2raw[:]))
                dve.tensor_copy(wn2[:, HI], w2wide[:]).then_inc(n2_hi, 1)
                dve.wait_ge(n2_hi, 1)
                minus(wn2[:, LO], w2wide[:], wn2[:, HI]).then_inc(n2_done, 1)
                dve.wait_ge(exp_done, 2)
                link(dve.tensor_scalar(exps[:], exps[:], 1.0, None, ALU.add))
                link(dve.reciprocal(decay[:], exps[:]))
                link(dve.tensor_tensor(bsum[:], bexp[:, 0], bexp[:, 1], ALU.add))
                link(dve.reciprocal(bsum[:], bsum[:]))
                for d in range(D):
                    link(stt(blend[:, d], bexp[:, d], 0.25, bsum[:], ALU.mult, ALU.mult))

            def add_identity(buf, k):
                block_k = buf[:, k * P:(k + 1) * P]
                dve.tensor_tensor(block_k, block_k, ident[:], ALU.add).then_inc(diag_done, 1)

            def split_weight(i):
                _, _, dst, scale = slices[i]
                dve.wait_ge(w_hi, i + 1)
                if scale == 1.0:
                    minus(dst[:, LO], stage[i % SLOTS], dst[:, HI]).then_inc(w_lo, 1)
                else:
                    stt(dst[:, LO], stage[i % SLOTS], scale, bits(dst[:, HI]), ALU.mult, ALU.subtract).then_inc(w_lo, 1)

            def x_low(n, some=range(KT)):
                for c in some:
                    need(dve, xh, n * KT + c + 1)
                    minus(xs_sgs[:, c, LO], xraw[:, c], xs_sgs[:, c, HI]).then_inc(xl, 1)

            def y_low(n):
                for o in range(KT):
                    need(dve, y_hi, n * KT + o + 1)
                    minus(ys[:, o, LO], y[:, o], ys[:, o, HI]).then_inc(y_lo, 1)

            def low_y0():
                for o in range(KT):
                    dve.wait_ge(y_hi, o + 1)
                    stt(ys[:, o, LO], psB[:, o], bsubj[:, 0, o:o + 1], bits(ys[:, o, HI]), ALU.add, ALU.subtract)\
                        .then_inc(y_lo, 1)

            def context(n, some):
                if 0 in some:
                    need(dve, ctx_kept, n * KT)
                    need(dve, bl_lo, n * KT)
                else:
                    need(dve, ctx_lo, n * KT + 2)
                for i in some:
                    c = CTX_ORDER[i]
                    dve.tensor_tensor_scan(tr0[:, c % 2], decay[:, 0:1].to_broadcast([P, N]), y[:, c],
                                           ctx_last[:, c:c + 1], ALU.mult, ALU.add).then_inc(ctx_raw, 1)
                for i in some:
                    c = CTX_ORDER[i]
                    need(dve, ctx_raw, n * KT + i + 1)
                    dve.tensor_copy(ctx_last[:, c:c + 1], tr0[:, c % 2, N - 1:N]).then_inc(ctx_kept, 1)
                    need(dve, ctx_hi, n * KT + i + 1)
                    minus(cts[:, c, LO], tr0[:, c % 2], cts[:, c, HI]).then_inc(ctx_lo, 1)

            def hidden(n):
                need(dve, h1_hi, n + 1)
                minus(h1s[:, LO], h1[:], h1s[:, HI]).then_inc(h1_lo, 1)

            def modulation(n):
                need(dve, mod_th, n + 1)
                dve.tensor_scalar(mod_row[:], mod_row[:], 2.0, None, ALU.add).then_inc(mod_two, 1)

            def blend_low(n, c):
                need(dve, bl_hi, n * KT + c + 1)
                minus(cts[:, tr_slot(c), LO], tr0[:, c % 2], cts[:, tr_slot(c), HI]).then_inc(bl_lo, 1)

            def turn(n, i):
                if i == 0:
                    need(dve, stored, n * KT * 16)
                else:
                    need(dve, res_in, n * RES_DMAS * 16 + i * QUADS * 16)
                for j in range(PAIR):
                    rows_j = y[:, :, (i * PAIR + j) * P:(i * PAIR + j + 1) * P]
                    dve.transpose(turning[:, :, j].rearrange("p b (k f) -> p b k f", k=KT),
                                  rows_j.rearrange("p k (t b) -> p b k t", b=P // QP)).then_inc(turned, 1)

            def traces(n, boundary=False):
                STEPS = 6
                need(dve, mod_done, (n + 1) * 16)
                need(dve, trace, n * KT * STEPS)
                need(dve, blended, n * KT)
                need(dve, ctx_lo, n * KT + KT)
                for c in range(KT):
                    s = c % 2
                    base = n * KT * STEPS + c * STEPS
                    need(dve, g_th, n * KT + c + 1)
                    if c >= 1:
                        need(dve, blended, n * KT + c)
                    stt(th[:, s], th[:, s], 1.0, y[:, c], ALU.add, ALU.mult).then_inc(gated, 1)
                    need(dve, gated, n * KT + c + 1)
                    if c >= 2:
                        need(dve, bl_lo, n * KT + c - 1)
                    stt(tr0[:, s], th[:, s], blend[:, 0, c:c + 1], mod[:, 0], ALU.mult, ALU.mult).then_inc(trace, 1)
                    stt(tr1[:], th[:, s], blend[:, 1, c:c + 1], mod[:, 1], ALU.mult, ALU.mult).then_inc(trace, 1)
                    if c >= 1:
                        blend_low(n, c - 1)
                    for d, buf in enumerate((tr0[:, s], tr1[:])):
                        dve.wait_ge(trace, base + d + 1)
                        dve.tensor_tensor_scan(buf, decay[:, 1 + d:2 + d].to_broadcast([P, N]), buf,
                                               tr_last[:, d, c:c + 1], ALU.mult, ALU.add).then_inc(trace, 1)
                    for d, buf in enumerate((tr0[:, s], tr1[:])):
                        dve.wait_ge(trace, base + D + d + 1)
                        dve.tensor_copy(tr_last[:, d, c:c + 1], buf[:, N - 1:N]).then_inc(trace, 1)
                    dve.wait_ge(trace, base + D + D + 1)
                    dve.tensor_tensor(tr0[:, s], tr0[:, s], tr1[:], ALU.add).then_inc(blended, 1)
                    if boundary and c == 1:
                        x_low(n + 1)
                    if c == 1:
                        turn(n, 1)
                blend_low(n, KT - 1)

            def soma_gate(n):
                need(dve, soma_done, n * KT + KT)
                for c in range(KT + 1):
                    if c < KT:
                        need(dve, t_th, n * KT + c + 1)
                        stt(gate_slots[c], gate_slots[c], 1.0, soma[:, c], ALU.add, ALU.mult).then_inc(sg_raw, 1)
                    if c >= 1:
                        need(dve, sg_hi, n * KT + c)
                        minus(xs_sgs[:, c - 1, LO], gate_slots[c - 1], xs_sgs[:, c - 1, HI]).then_inc(sg_lo, 1)

            def norm(n, last=False):
                def stats_of(j):
                    need(dve, o_mm, n * KT + j + 1)
                    dve.bn_stats(stats[:, j], psA[:, j]).then_inc(ln_stats, 1)

                def aggregate(j):
                    dve.bn_aggr(mv[:, j], stats[:, j]).then_inc(ln_mv, 1)

                def centre(j):
                    need(dve, ln_mv, n * KT + j + 1)
                    stt(normed[:, j % 2], psA[:, j], mv[:, j, 0:1], gamma_b[:], ALU.subtract, ALU.mult)\
                        .then_inc(ln_centred, 1)

                def finish(j):
                    need(dve, ln_centred, n * KT + j + 1)
                    need(dve, res_beta, n * KT + j + 1)
                    need(dve, ln_rstd, n * KT + j + 1)
                    stt(res[:, j], normed[:, j % 2], rstd[:, j:j + 1], res[:, j], ALU.mult, ALU.add)\
                        .then_inc(result, 1)

                need(dve, ln_rstd, n * KT)
                need(dve, sg_lo, n * KT + KT)
                if last:
                    stats_of(0)
                    for j in range(KT):
                        dve.wait_ge(ln_stats, n * KT + j + 1)
                        aggregate(j)
                        if j >= 2:
                            dve.wait_ge(result, n * KT + j - 1)
                        centre(j)
                        if j + 1 < KT:
                            stats_of(j + 1)
                        finish(j)
                    return
                stats_of(0)
                for j in range(1, KT):
                    need(dve, ln_stats, n * KT + j)
                    stats_of(j)
                    aggregate(j - 1)
                    if j >= 3:
                        need(dve, result, n * KT + j - 2)
                    centre(j - 1)
                    if j == 2:
                        finish(0)
                need(dve, ln_stats, n * KT + KT)
                finish(1)
                aggregate(KT - 1)
                need(dve, result, n * KT + 2)
                centre(KT - 1)
                finish(2)
                finish(3)

            def second_weights_low():
                for k in range(KT):
                    dve.wait_ge(w1_hi, k + 1)
                    minus(wl0[:, k, LO], xraw[:, k], wl0[:, k, HI]).then_inc(w1_lo, 1)
                dve.wait_ge(ctx_kept, TPB * KT)
                link(dve.memset(ctx_last[:], 0.0))

            def step(n, last=False, boundary=False):
                if boundary:
                    second_weights_low()
                elif not last:
                    x_low(n + 1)
                turn(n, 0)
                traces(n, boundary)
                if not last:
                    y_low(n + 1)
                    context(n + 1, (0, 1))
                soma_gate(n)
                if not last:
                    hidden(n + 1)
                    context(n + 1, (2, 3))
                norm(n, last)
                if not last:
                    modulation(n + 1)

            dve.wait_ge(ident_done, 1)
            for k in range(KT):
                dve.wait_ge(stage_in[k], 16)
                add_identity(stage[k], k)
                x_low(0, (k,))
                split_weight(k)
                if k == 1:
                    small_constants()
            for i in range(AT_N1, AT_SOMA + 3):
                split_weight(i)
            dve.wait_ge(bsubj_in, 16 * BATCH)
            low_y0()
            split_weight(AT_SOMA + 3)
            split_weight(AT_G)
            decays_and_blend()
            hidden(0)
            for i in range(1, 5):
                split_weight(AT_G + i)
            dve.wait_ge(y0_sum, KT)
            context(0, (0, 1))
            for i in range(5, 8):
                split_weight(AT_G + i)
            modulation(0)
            context(0, (2, 3))
            for i in range(AT_TEMP, END):
                split_weight(i)
            dve.wait_ge(w_lo, END)
            step(0)
            with dve.Fori(1, 3) as n:
                step(n)
            dve.wait_ge(w1_in, 16)
            for k in range(KT):
                add_identity(xraw[:, k], k)

            step(3, boundary=True)
            dve.wait_ge(trace, TPB * KT * 6)
            link(dve.memset(tr_last[:], 0.0))
            with dve.Fori(4, TILES - 1) as n:
                step(n)
            step(TILES - 1, last=True)


def kernel(x, itok_B_0_7, condB_tauraws, cond_256, condB_bn2, cond_1024, L0_cond_weight, L0_cond_bias,
           L1_cond_tau_ctx, L1_cond_Wg, L1_cond_bg, L1_cond_Wn1, L1_cond_bn1, L1_cond_Wsoma, L1_cond_bsoma,
           L1_cond_Wtemp, L1_cond_btemp, L1_cond_Wout, L1_cond_gamma, L1_cond_beta):
    import numpy as np
    import concourse.bacc as bacc
    from concourse.bass_utils import run_bass_kernel_spmd

    def tiled(a, axis):
        a = np.moveaxis(np.asarray(a), axis, -1)
        a = a.reshape(*a.shape[:-1], -1, QUADS, KT, QP).swapaxes(-3, -2).reshape(a.shape)
        return np.moveaxis(a, -1, axis)

    def rows(w):
        w = tiled(w, 1)
        return np.ascontiguousarray(w.T.reshape(-1, P, w.shape[0]))

    def chan(v):
        return tiled(v, 0).reshape(-1, P).T

    subj = tiled(tiled(L0_cond_weight, 1), 2)
    arrays = {
        "x_t": np.ascontiguousarray(tiled(x, 2).reshape(TILES, N, KT, P).transpose(0, 3, 2, 1)),
        "ids": np.asarray(itok_B_0_7).reshape(1, BATCH),
        "w_subj": np.ascontiguousarray(subj.transpose(0, 2, 1).reshape(subj.shape[0], KT, P, E)),
        "b_subj": np.ascontiguousarray(tiled(L0_cond_bias, 1).reshape(-1, KT, P).transpose(0, 2, 1)),
        "w_g": rows(tiled(L1_cond_Wg, 0)),
        "w_n1": np.ascontiguousarray(rows(L1_cond_Wn1).transpose(1, 0, 2).reshape(1, P, E)),
        "w_n2": np.ascontiguousarray(np.asarray(cond_256).T),
        "w_soma": rows(tiled(L1_cond_Wsoma, 0)),
        "w_temp": rows(tiled(L1_cond_Wtemp, 0)),
        "w_out": rows(L1_cond_Wout),
        "vecs": np.ascontiguousarray(np.concatenate(
            [chan(L1_cond_bg), chan(L1_cond_bsoma), chan(L1_cond_btemp), np.asarray(L1_cond_bn1).reshape(P, 1),
             *[chan(row) for row in np.asarray(cond_1024)]], axis=1)),
        "scal": np.concatenate([np.asarray(L1_cond_tau_ctx).reshape(1), np.asarray(condB_tauraws)]),
        "bn_2": np.asarray(condB_bn2).reshape(D, 1),
        "gamma": np.asarray(L1_cond_gamma),
        "beta": np.asarray(L1_cond_beta),
    }
    nc = bacc.Bacc("TRN2", target_bir_lowering=False, num_devices=1, dynamic_dma_scratch_size=1024)
    aps = {k: nc.dram_tensor(f"in_{k}", a.shape, mybir.dt.from_np(a.dtype), kind="ExternalInput").ap()
           for k, a in arrays.items()}
    out = nc.dram_tensor("out_0", (BATCH, SEQ, E), F32, kind="ExternalOutput").ap()
    build(nc, **aps, out=out)
    r = run_bass_kernel_spmd(nc, [{f"in_{k}": a for k, a in arrays.items()}], core_ids=[0])
    return r.results[0]["out_0"]
```
